# Optimizing a Trainium2 kernel written in Bass

```python
import numpy as np
import jax
import jax.numpy as jnp

def _softmax(x, axis=-1):
    return jax.nn.softmax(x, axis=axis)

def _gelu(x):
    return jax.nn.gelu(x, approximate=True)

def _silu(x):
    return jax.nn.silu(x)

def _sigmoid(x):
    return jax.nn.sigmoid(x)

def _layernorm(x, axis=-1, eps=1e-05):
    m = jnp.mean(x, axis=axis, keepdims=True)
    v = jnp.var(x, axis=axis, keepdims=True)
    return (x - m) / jnp.sqrt(v + eps)

def _scatter_add(tgt, idx, src, axis=0):
    return tgt.at[idx].add(src)

def _segment_sum(src, seg, n):
    return jax.ops.segment_sum(src, seg, n)
kernel_name = 'mk_gnn_preln_d4_gnn_r8_53c9c9'

def setup_inputs(seed: int=0):
    np.random.seed(seed)
    _w = jnp.asarray

    def _rec_inputs():
        import jax
        import jax.numpy as jnp
        _gk = jax.random.key(seed)
        x = 0.0004528 + 0.9998 * jax.random.normal(jax.random.fold_in(_gk, 1), (12500, 16), jnp.float32)
        src = jax.random.randint(jax.random.fold_in(_gk, 2), (400000,), 0, 12500, jnp.int32)
        dst = jnp.minimum((12500 * jax.random.uniform(jax.random.fold_in(_gk, 3), (400000,)) ** 2.0).astype(jnp.int32), 99999)
        _o = jnp.argsort(dst, stable=True)
        src = src[_o]
        dst = dst[_o]
        edge_attr_8 = -5.3897e-05 + 0.999841 * jax.random.normal(jax.random.fold_in(_gk, 12), (400000, 8), jnp.float32)
        edge_type_8 = jax.random.randint(jax.random.fold_in(_gk, 14), (400000,), 0, 8, jnp.int32)
        node_vec1 = -0.00472126 + 0.997171 * jax.random.normal(jax.random.fold_in(_gk, 15), (12500, 1), jnp.float32)
        return (x, src, dst, edge_attr_8, edge_type_8, node_vec1)
    x, src, dst, edge_attr_8, edge_type_8, node_vec1 = _rec_inputs()

    def _L0_gnn_setup():
        import jax, jax.numpy as jnp
        import numpy as np
        NUM_ENTITIES = 12500
        NUM_RELATIONS = 8
        NUM_CLASSES = 16
        HIDDEN = 16
        NUM_EDGES = 400000

        def rgcn_conv(x, src, dst, edge_type, W, root, bias):
            num_nodes = x.shape[0]
            x_src = x[src]
            msg = jnp.zeros((src.shape[0], W.shape[2]), x.dtype)
            for r in range(NUM_RELATIONS):
                msg = msg + jnp.where((edge_type == r)[:, None], x_src @ W[r], jnp.zeros((), x.dtype))
            cnt = jnp.zeros((num_nodes, NUM_RELATIONS), x.dtype).at[dst, edge_type].add(1.0)
            norm = 1.0 / jnp.maximum(cnt[dst, edge_type], 1.0)
            agg = jax.ops.segment_sum(msg * norm[:, None], dst, num_segments=num_nodes)
            return agg + x @ root + bias
        key = jax.random.key(seed)
        ks = jax.random.split(key, 9)
        s = 1.0 / np.sqrt(HIDDEN)
        edge_index = jax.random.randint(ks[0], (2, NUM_EDGES), 0, NUM_ENTITIES, dtype=jnp.int32)
        edge_type = jax.random.randint(ks[1], (NUM_EDGES,), 0, NUM_RELATIONS, dtype=jnp.int32)
        return {'embed': jax.random.normal(ks[2], (NUM_ENTITIES, HIDDEN), jnp.float32), 'W1': jax.random.normal(ks[3], (NUM_RELATIONS, HIDDEN, HIDDEN), jnp.float32) * s, 'root1': jax.random.normal(ks[4], (HIDDEN, HIDDEN), jnp.float32) * s, 'b1': jnp.zeros((HIDDEN,), jnp.float32), 'W2': jax.random.normal(ks[5], (NUM_RELATIONS, HIDDEN, NUM_CLASSES), jnp.float32) * s, 'root2': jax.random.normal(ks[6], (HIDDEN, NUM_CLASSES), jnp.float32) * s, 'b2': jnp.zeros((NUM_CLASSES,), jnp.float32), 'edge_index': edge_index, 'edge_type': edge_type}
    _L0_gnn_all = _L0_gnn_setup()
    _L0_gnn_in = {k: v for k, v in _L0_gnn_all.items() if k in ('W1', 'root1', 'b1', 'W2', 'root2', 'b2')}
    del _L0_gnn_all

    def _L1_gnn_setup():
        import jax, jax.numpy as jnp
        import numpy as np
        N_NODES = 12500
        N_EDGES = 400000
        NUM_REL = 8

        def _rgcn_layer(x, src, dst, edge_type, W, root, bias):
            out = x @ root + bias
            x_src = x[src]
            for r in range(W.shape[0]):
                mask = (edge_type == r).astype(x.dtype)
                s = jax.ops.segment_sum(x_src * mask[:, None], dst, num_segments=x.shape[0])
                cnt = jax.ops.segment_sum(mask, dst, num_segments=x.shape[0])
                agg = s / jnp.clip(cnt, 1.0)[:, None]
                out = out + agg @ W[r]
            return out
        key = jax.random.key(seed)
        ks = jax.random.split(key, 9)
        x = jax.random.normal(ks[0], (N_NODES, 16), dtype=jnp.float32)
        edge_index = jax.random.randint(ks[1], (2, N_EDGES), 0, N_NODES, dtype=jnp.int32)
        edge_type = jax.random.randint(ks[2], (N_EDGES,), 0, NUM_REL, dtype=jnp.int32)
        s1 = 1.0 / np.sqrt(16.0)
        s2 = 1.0 / np.sqrt(32.0)
        W1 = jax.random.normal(ks[3], (NUM_REL, 16, 32), dtype=jnp.float32) * s1
        root1 = jax.random.normal(ks[4], (16, 32), dtype=jnp.float32) * s1
        b1 = jnp.zeros((32,), dtype=jnp.float32)
        W2 = jax.random.normal(ks[5], (NUM_REL, 32, 16), dtype=jnp.float32) * s2
        root2 = jax.random.normal(ks[6], (32, 16), dtype=jnp.float32) * s2
        b2 = jnp.zeros((16,), dtype=jnp.float32)
        return {'x': x, 'edge_index': edge_index, 'edge_type': edge_type, 'W1': W1, 'root1': root1, 'b1': b1, 'W2': W2, 'root2': root2, 'b2': b2}
    _L1_gnn_all = _L1_gnn_setup()
    _L1_gnn_in = {k: v for k, v in _L1_gnn_all.items() if k in ('W1', 'root1', 'b1', 'W2', 'root2', 'b2')}
    del _L1_gnn_all

    def _L2_gnn_setup():
        import jax, jax.numpy as jnp
        import numpy as np
        N_NODES = 12500
        N_EDGES = 400000
        D_NODE = 16
        D_EDGE = 8
        D_HIDDEN = 16
        key = jax.random.key(seed)
        ks = jax.random.split(key, 8)
        node_features = jax.random.normal(ks[0], (N_NODES, D_NODE), dtype=jnp.float32)
        edge_attr_e3nn = jax.random.normal(ks[1], (N_EDGES, D_EDGE), dtype=jnp.float32)
        node_attr_scalar_raw = jax.random.normal(ks[2], (N_NODES, 1), dtype=jnp.float32)
        W_msg_tp = jax.random.normal(ks[3], (D_NODE, D_EDGE, D_HIDDEN), dtype=jnp.float32)
        W_msg_lin = jax.random.normal(ks[4], (D_HIDDEN, D_HIDDEN), dtype=jnp.float32)
        W_upd_tp = jax.random.normal(ks[5], (D_NODE, D_HIDDEN, D_HIDDEN), dtype=jnp.float32)
        W_upd_lin = jax.random.normal(ks[6], (D_HIDDEN, D_NODE), dtype=jnp.float32)
        edge_index = jax.random.randint(ks[7], (2, N_EDGES), 0, N_NODES, dtype=jnp.int64)
        return {'node_features': node_features, 'edge_attr_e3nn': edge_attr_e3nn, 'node_attr_scalar_raw': node_attr_scalar_raw, 'W_msg_tp': W_msg_tp, 'W_msg_lin': W_msg_lin, 'W_upd_tp': W_upd_tp, 'W_upd_lin': W_upd_lin, 'edge_index': edge_index}
    _L2_gnn_all = _L2_gnn_setup()
    _L2_gnn_in = {k: v for k, v in _L2_gnn_all.items() if k in ('W_msg_tp', 'W_msg_lin', 'W_upd_tp', 'W_upd_lin')}
    del _L2_gnn_all

    def _L3_gnn_setup():
        import jax, jax.numpy as jnp
        import numpy as np
        N_NODES = 12500
        N_EDGES = 125000
        MSG_DIM = 16
        HID_DIM = 16
        N_EDGE_TYPE = 8
        key = jax.random.key(seed)
        ks = jax.random.split(key, 9)
        features = jax.random.normal(ks[0], (N_NODES, HID_DIM), dtype=jnp.float32)
        edge_src = jax.random.randint(ks[1], (N_EDGES,), 0, N_NODES, dtype=jnp.int32)
        edge_dst = jax.random.randint(ks[2], (N_EDGES,), 0, N_NODES, dtype=jnp.int32)
        edge_type = jax.random.randint(ks[3], (N_EDGES,), 0, N_EDGE_TYPE, dtype=jnp.int32)
        edge_emb = jax.random.normal(ks[4], (N_EDGE_TYPE, MSG_DIM * HID_DIM), dtype=jnp.float32) * 0.1
        s = 1.0 / np.sqrt(HID_DIM)
        w_ih = jax.random.uniform(ks[5], (3 * HID_DIM, MSG_DIM), minval=-s, maxval=s, dtype=jnp.float32)
        w_hh = jax.random.uniform(ks[6], (3 * HID_DIM, HID_DIM), minval=-s, maxval=s, dtype=jnp.float32)
        b_ih = jax.random.uniform(ks[7], (3 * HID_DIM,), minval=-s, maxval=s, dtype=jnp.float32)
        b_hh = jax.random.uniform(ks[8], (3 * HID_DIM,), minval=-s, maxval=s, dtype=jnp.float32)
        return {'features': features, 'edge_src': edge_src, 'edge_dst': edge_dst, 'edge_type': edge_type, 'edge_emb': edge_emb, 'w_ih': w_ih, 'w_hh': w_hh, 'b_ih': b_ih, 'b_hh': b_hh}
    _L3_gnn_all = _L3_gnn_setup()
    _L3_gnn_in = {k: v for k, v in _L3_gnn_all.items() if k in ('edge_emb', 'w_ih', 'w_hh', 'b_ih', 'b_hh')}
    del _L3_gnn_all
    return {'x': x, 'src': src, 'dst': dst, 'edge_attr_8': edge_attr_8, 'edge_type_8': edge_type_8, 'node_vec1': node_vec1, 'L0_gnn_W1': _L0_gnn_in['W1'], 'L0_gnn_root1': _L0_gnn_in['root1'], 'L0_gnn_b1': _L0_gnn_in['b1'], 'L0_gnn_W2': _L0_gnn_in['W2'], 'L0_gnn_root2': _L0_gnn_in['root2'], 'L0_gnn_b2': _L0_gnn_in['b2'], 'L1_gnn_W1': _L1_gnn_in['W1'], 'L1_gnn_root1': _L1_gnn_in['root1'], 'L1_gnn_b1': _L1_gnn_in['b1'], 'L1_gnn_W2': _L1_gnn_in['W2'], 'L1_gnn_root2': _L1_gnn_in['root2'], 'L1_gnn_b2': _L1_gnn_in['b2'], 'L2_gnn_W_msg_tp': _L2_gnn_in['W_msg_tp'], 'L2_gnn_W_msg_lin': _L2_gnn_in['W_msg_lin'], 'L2_gnn_W_upd_tp': _L2_gnn_in['W_upd_tp'], 'L2_gnn_W_upd_lin': _L2_gnn_in['W_upd_lin'], 'L3_gnn_edge_emb': _L3_gnn_in['edge_emb'], 'L3_gnn_w_ih': _L3_gnn_in['w_ih'], 'L3_gnn_w_hh': _L3_gnn_in['w_hh'], 'L3_gnn_b_ih': _L3_gnn_in['b_ih'], 'L3_gnn_b_hh': _L3_gnn_in['b_hh']}

def reference(x, src, dst, edge_attr_8, edge_type_8, node_vec1, L0_gnn_W1, L0_gnn_root1, L0_gnn_b1, L0_gnn_W2, L0_gnn_root2, L0_gnn_b2, L1_gnn_W1, L1_gnn_root1, L1_gnn_b1, L1_gnn_W2, L1_gnn_root2, L1_gnn_b2, L2_gnn_W_msg_tp, L2_gnn_W_msg_lin, L2_gnn_W_upd_tp, L2_gnn_W_upd_lin, L3_gnn_edge_emb, L3_gnn_w_ih, L3_gnn_w_hh, L3_gnn_b_ih, L3_gnn_b_hh):
    import jax
    import jax.numpy as jnp

    def _L0_gnn_ref(embed, W1, root1, b1, W2, root2, b2, edge_index, edge_type):
        import jax, jax.numpy as jnp
        import numpy as np
        NUM_ENTITIES = 12500
        NUM_RELATIONS = 8
        NUM_CLASSES = 16
        HIDDEN = 16
        NUM_EDGES = 400000

        def rgcn_conv(x, src, dst, edge_type, W, root, bias):
            num_nodes = x.shape[0]
            x_src = x[src]
            msg = jnp.zeros((src.shape[0], W.shape[2]), x.dtype)
            for r in range(NUM_RELATIONS):
                msg = msg + jnp.where((edge_type == r)[:, None], x_src @ W[r], jnp.zeros((), x.dtype))
            cnt = jnp.zeros((num_nodes, NUM_RELATIONS), x.dtype).at[dst, edge_type].add(1.0)
            norm = 1.0 / jnp.maximum(cnt[dst, edge_type], 1.0)
            agg = jax.ops.segment_sum(msg * norm[:, None], dst, num_segments=num_nodes)
            return agg + x @ root + bias
        src, dst = (edge_index[0], edge_index[1])
        h = rgcn_conv(embed, src, dst, edge_type, W1, root1, b1)
        h = jax.nn.relu(h)
        h = rgcn_conv(h, src, dst, edge_type, W2, root2, b2)
        return jax.nn.log_softmax(h, axis=1)

    def _L1_gnn_ref(x, edge_index, edge_type, W1, root1, b1, W2, root2, b2):
        import jax, jax.numpy as jnp
        import numpy as np
        N_NODES = 12500
        N_EDGES = 400000
        NUM_REL = 8

        def _rgcn_layer(x, src, dst, edge_type, W, root, bias):
            out = x @ root + bias
            x_src = x[src]
            for r in range(W.shape[0]):
                mask = (edge_type == r).astype(x.dtype)
                s = jax.ops.segment_sum(x_src * mask[:, None], dst, num_segments=x.shape[0])
                cnt = jax.ops.segment_sum(mask, dst, num_segments=x.shape[0])
                agg = s / jnp.clip(cnt, 1.0)[:, None]
                out = out + agg @ W[r]
            return out
        src, dst = (edge_index[0], edge_index[1])
        h = _rgcn_layer(x, src, dst, edge_type, W1, root1, b1)
        h = jax.nn.relu(h)
        h = _rgcn_layer(h, src, dst, edge_type, W2, root2, b2)
        return h

    def _L2_gnn_ref(node_features, edge_attr_e3nn, node_attr_scalar_raw, W_msg_tp, W_msg_lin, W_upd_tp, W_upd_lin, edge_index):
        import jax, jax.numpy as jnp
        import numpy as np
        N_NODES = 12500
        N_EDGES = 400000
        D_NODE = 16
        D_EDGE = 8
        D_HIDDEN = 16
        n_nodes = node_features.shape[0]
        row = edge_index[0]
        col = edge_index[1]
        norm_msg_tp = 1.0 / np.float32(np.sqrt(D_NODE * D_EDGE))
        norm_upd_tp = 1.0 / np.float32(np.sqrt(D_NODE * D_HIDDEN))
        norm_lin = 1.0 / np.float32(np.sqrt(D_HIDDEN))
        x_j = node_features[col]
        m = jnp.einsum('ei,ej,ijh->eh', x_j, edge_attr_e3nn, W_msg_tp) * norm_msg_tp
        m = jax.nn.silu(m)
        m = m @ W_msg_lin * norm_lin
        agg = jax.ops.segment_sum(m, row, num_segments=n_nodes)
        u = jnp.einsum('ni,nh,ihk->nk', node_features, agg, W_upd_tp) * norm_upd_tp
        u = jax.nn.silu(u)
        u = u @ W_upd_lin * norm_lin
        return node_features + u

    def _L3_gnn_ref(features, edge_src, edge_dst, edge_type, edge_emb, w_ih, w_hh, b_ih, b_hh):
        import jax, jax.numpy as jnp
        import numpy as np
        N_NODES = 12500
        N_EDGES = 125000
        MSG_DIM = 16
        HID_DIM = 16
        N_EDGE_TYPE = 8
        n_nodes = features.shape[0]
        A = edge_emb[edge_type].reshape(-1, MSG_DIM, HID_DIM)
        h_src = features[edge_src]
        msg = jnp.einsum('emh,eh->em', A, h_src)
        m = jax.ops.segment_sum(msg, edge_dst, num_segments=n_nodes)
        gi = m @ w_ih.T + b_ih
        gh = features @ w_hh.T + b_hh
        i_r, i_z, i_n = jnp.split(gi, 3, axis=-1)
        h_r, h_z, h_n = jnp.split(gh, 3, axis=-1)
        r = jax.nn.sigmoid(i_r + h_r)
        z = jax.nn.sigmoid(i_z + h_z)
        n = jnp.tanh(i_n + r * h_n)
        h_new = (1.0 - z) * n + z * features
        return h_new
    edge_index = jnp.stack([src, dst])
    h = jnp.maximum(_layernorm(x, axis=-1), 0.0)
    x = x + _L0_gnn_ref(h, L0_gnn_W1, L0_gnn_root1, L0_gnn_b1, L0_gnn_W2, L0_gnn_root2, L0_gnn_b2, edge_index, edge_type_8)
    h = jnp.maximum(_layernorm(x, axis=-1), 0.0)
    x = x + _L1_gnn_ref(h, edge_index, edge_type_8, L1_gnn_W1, L1_gnn_root1, L1_gnn_b1, L1_gnn_W2, L1_gnn_root2, L1_gnn_b2)
    h = jnp.maximum(_layernorm(x, axis=-1), 0.0)
    x = x + _L2_gnn_ref(h, edge_attr_8, node_vec1, L2_gnn_W_msg_tp, L2_gnn_W_msg_lin, L2_gnn_W_upd_tp, L2_gnn_W_upd_lin, edge_index)
    h = jnp.maximum(_layernorm(x, axis=-1), 0.0)
    x = x + _L3_gnn_ref(h, src, dst, edge_type_8, L3_gnn_edge_emb, L3_gnn_w_ih, L3_gnn_w_hh, L3_gnn_b_ih, L3_gnn_b_hh)
    return x

_drawn_inputs = setup_inputs


def setup_inputs(seed=0):
    import zlib

    import numpy as np

    out = dict(_drawn_inputs(seed))
    spreads = {'L0_gnn_b1': (0.0, 0.1),
     'L0_gnn_b2': (0.0, 0.1),
     'L1_gnn_b1': (0.0, 0.1),
     'L1_gnn_b2': (0.0, 0.678)}
    factors = {'L3_gnn_w_hh': 2.967, 'L3_gnn_b_ih': 4.896, 'L3_gnn_b_hh': 8.0}
    for name, (base, spread) in spreads.items():
        noise = np.random.default_rng([zlib.crc32(name.encode()), seed]).standard_normal(out[name].shape)
        drawn = base * np.exp(spread * noise) if base else spread * noise
        out[name] = jnp.asarray(drawn.astype(out[name].dtype))
    for name, factor in factors.items():
        out[name] = (out[name] * factor).astype(out[name].dtype)
    return out
```

```python
from contextlib import ExitStack

import concourse.bass as bass
from concourse import mybir

F32 = mybir.dt.float32
I32 = mybir.dt.int32
ALU = mybir.AluOpType
ACT = mybir.ActivationFunctionType
AX = mybir.AxisListType

P = 128
NODES = 12500
EDGES = 400000
F = 16
R = 8
WINDOWS = -(-NODES // P)
NPAD = WINDOWS * P
TAIL = NODES - (WINDOWS - 1) * P
G = 16
GE = G * P
SLOTS = 4
TURNS = -(-EDGES // (GE * SLOTS))
GROUPS = TURNS * SLOTS
EPAD = GROUPS * GE
EC = EPAD // P
FIELDS = 6
SRC_ROW, DST_ROW, TYPE_ROW, DST, TYPE, SRC = range(FIELDS)
REC = FIELDS * G
CHUNKS = 4
CG = GROUPS // CHUNKS
RF = R * F
SW = RF + R
NB = 7
BATCHES = WINDOWS // NB
LANDED = 16 * G
EPS = 1e-5
PASSES = 6
CONV = [0, 1, 2, 3, 5]
TP = 4
WEIGHTS = [("a1", 128, 16), ("ar1", 16, 16), ("a2", 128, 16), ("ar2", 16, 16), ("b1", 128, 32), ("br1", 16, 32),
           ("b2", 32, 128), ("br2", 32, 16), ("mtp", 128, 16), ("mlin", 16, 16), ("utp0", 128, 16), ("utp1", 128, 16),
           ("ulin", 16, 16), ("emb", 128, 16), ("gi", 16, 64), ("gh", 16, 64)]
BIASES = [("ab1", 16), ("ab2", 16), ("bb1", 32), ("bb2", 16), ("ih", 48), ("hh", 48)]


def places(list_of_sizes):
    at, found = 0, {}
    for name, *_, n in list_of_sizes:
        found[name] = (at, n)
        at += n
    return found, at


def gnn_kernel(nc, x, src, dst, typ, src_flat, attr, w, biases, out):
    WP, WCOLS = places(WEIGHTS)
    BP, BCOLS = places(BIASES)
    with ExitStack() as ctx:
        def sb(name, shape, dt=F32):
            return ctx.enter_context(nc.sbuf_tensor(name, shape, dt))

        def ps(name, shape):
            return ctx.enter_context(nc.psum_tensor(name, shape, F32))

        def sem(name):
            return ctx.enter_context(nc.semaphore(name))

        def sems(name, n):
            return [sem(f"{name}{i}") for i in range(n)]

        table = {p: nc.dram_tensor(f"table{p}", (NPAD, F), F32, kind="Internal").ap() for p in range(PASSES) if p != 3}
        table[3] = nc.dram_tensor("table3", (NPAD * R, F), F32, kind="Internal").ap()
        records = nc.dram_tensor("records", (P, GROUPS * REC), I32, kind="Internal").ap()
        sums = [nc.dram_tensor(f"sums{i}", (NPAD + P, F), F32, kind="Internal").ap() for i in range(G)]

        xs = sb("xs", [P, WINDOWS, F])
        hs = sb("hs", [P, WINDOWS * 2 * F])
        S = sb("S", [P, WINDOWS, SW])
        ta = sb("ta", [P, WINDOWS * 2 * F])
        tb = sb("tb", [P, WINDOWS * F])
        inv = sb("inv", [P, WINDOWS, R])
        stat = sb("stat", [P, 2, WINDOWS])
        rec = sb("rec", [P, SLOTS, FIELDS, G], I32)
        rows = sb("rows", [P, SLOTS, G, F])
        expanded = sb("expanded", [P, 2, G, SW])
        onehot = sb("onehot", [P, G, P])
        rel = sb("rel", [P, G])
        iota_n = sb("iota_n", [P, P])
        iota_r = sb("iota_r", [P, R])
        ident = sb("ident", [P, P])
        before = sb("before", [P, P])
        spare = sb("spare", [P, 1])
        start_of = sb("start_of", [P, WINDOWS])
        wt = sb("wt", [P, WCOLS])
        bt = sb("bt", [P, BCOLS])
        bg = sb("bg", [P, 4 * F])
        na = sb("na", [P, NB * P])
        nb = sb("nb", [P, NB * 2 * F])
        nat = sb("nat", [P, NB * P])
        nbt = sb("nbt", [P, NB * P])
        ext = sb("ext", [P, 2, GROUPS])
        extr = sb("extr", [P, 2, GROUPS])
        span = sb("span", [1, 6, GROUPS])
        spans = sb("spans", [1, GROUPS, 4], I32)
        attrs = sb("attrs", [P, SLOTS, G, R])
        msg = sb("msg", [P, 2, G * F])
        summed = sb("summed", [P, SLOTS, G * F])
        scat = sb("scat", [P, SLOTS, G], I32)
        dup = sb("dup", [P, 3, G])

        psA = ps("psA", [P, 2048])
        psB = ps("psB", [P, 1024])
        psC = ps("psC", [P, 512])

        flatS = S[:, :, :].rearrange("p w f -> p (w f)")
        srcs = flatS[:, 0:SLOTS * GE].bitcast(I32).rearrange("p (s e) -> p s e", s=SLOTS)
        outerT = flatS[:, SLOTS * GE:SLOTS * GE + GE]
        earlier = flatS[:, (SLOTS + 1) * GE:(SLOTS + 2) * GE].rearrange("p (t e) -> p t e", t=G)

        def W(name):
            rows_of = {n: k for n, k, _ in WEIGHTS}
            at, n = WP[name]
            return wt[0:rows_of[name], at:at + n]

        def B(name, lo=0, hi=None):
            at, n = BP[name]
            return bt[:, at + lo:at + (n if hi is None else hi)]

        constants_in = sem("constants_in")
        x_in = sem("x_in")
        iotas = sem("iotas")
        edges_in = sems("edges_in", CHUNKS)
        records_built = sem("records_built")
        records_out = sems("records_out", CHUNKS)
        ext_ready = sem("ext_ready")
        extr_ready = sem("extr_ready")
        spans_ready = sem("spans_ready")
        cleared = sem("cleared")
        sums_zero = sem("sums_zero")
        dve_steps = sem("dve_steps")
        act_asked = sem("act_asked")
        act_done = sem("act_done")
        h_ready = sem("h_ready")
        table_out = sem("table_out")
        slot_free = sems("slot_free", SLOTS)
        rec_in = sems("rec_in", SLOTS)
        rows_in = [sems(f"rows_in_{k}_", SLOTS) for k in range(PASSES // 3)]
        masks_ready = sem("masks_ready")
        groups_begun = sem("groups_begun")
        expanded_ready = sems("expanded_ready", SLOTS)
        rel_ready = {p: sem(f"rel_ready{p}") for p in CONV}
        onehot_ready = {p: sem(f"onehot_ready{p}") for p in CONV}
        pair_done = {p: sem(f"pair_done{p}") for p in CONV}
        operands_ready = sem("operands_ready")
        turned = sem("turned")
        turned_out = sem("turned_out")
        product_done = sem("product_done")
        batch_done = sem("batch_done")
        attrs_in = sems("attrs_in", SLOTS)
        srcs_in = sems("srcs_in", SLOTS)
        outer_turned = sem("outer_turned")
        outer_out = sem("outer_out")
        msg_product = sem("msg_product")
        msg_ready = sem("msg_ready")
        same_ready = sem("same_ready")
        same_summed = sem("same_summed")
        summed_ready = sems("summed_ready", SLOTS)
        scattered = sems("scattered", SLOTS)
        scatter_free = sems("scatter_free", SLOTS)
        dup_steps = sem("dup_steps")
        sums_scattered = sem("sums_scattered")
        sums_in = sems("sums_in", 2)
        sums_read = sem("sums_read")
        out_ready = sem("out_ready")
        out_done = sem("out_done")

        n_constants = 16 * (len(WEIGHTS) + 2 + len(BIASES))

        def within(v, hi):
            return nc.s_assert_within(v, 0, hi, skip_runtime_bounds_check_because="the tables of spans hold windows alone")

        block = ctx.enter_context(nc.Block())

        def edge_chunk(c):
            return flatS[:, 0:3 * CG * G].bitcast(I32).rearrange("p (k e) -> p k e", k=3)

        def record_chunk(c):
            at = 3 * CG * G + (c % 2) * CG * REC
            return flatS[:, at:at + CG * REC].bitcast(I32).rearrange("p (g k t) -> p g k t", g=CG, k=FIELDS)

        def store_records(sp, c):
            sp.wait_ge(records_built, c + 1)
            sp.dma_start(records[:, c * CG * REC:(c + 1) * CG * REC],
                         record_chunk(c).rearrange("p g k t -> p (g k t)")).then_inc(records_out[c], 16)

        @block.sync
        def _(sp):
            sp.dma_start(xs[:, 0:WINDOWS - 1, :], x[0:(WINDOWS - 1) * P, :].rearrange("(w p) f -> p w f", p=P)).then_inc(x_in, 16)
            sp.wait_ge(cleared, 2)
            sp.dma_start(xs[0:TAIL, WINDOWS - 1, :], x[(WINDOWS - 1) * P:NODES, :]).then_inc(x_in, 16)
            for c in range(CHUNKS):
                if c:
                    store_records(sp, c - 1)
                for i, a in enumerate((src, dst, typ)):
                    sp.dma_start(edge_chunk(c)[:, i, :], a[:, c * CG * G:(c + 1) * CG * G]).then_inc(edges_in[c], 16)
                if c == 0:
                    for name, k, n in WEIGHTS:
                        if name in ("gi", "gh"):
                            at, _n = WP[name]
                            sp.dma_start(wt[0:F, at:at + 2 * F], w[name][:, 0:2 * F]).then_inc(constants_in, 16)
                            to = at + 2 * F if name == "gi" else at + 3 * F
                            sp.dma_start(wt[0:F, to:to + F], w[name][:, 2 * F:3 * F]).then_inc(constants_in, 16)
                        else:
                            sp.dma_start(W(name), w[name]).then_inc(constants_in, 16)
                    for name, n in BIASES:
                        sp.dma_start(B(name), biases[name].partition_broadcast(P)).then_inc(constants_in, 16)
            store_records(sp, CHUNKS - 1)
            sp.wait_ge(cleared, 3)
            for i in range(G):
                sp.dma_start(sums[i].rearrange("(p t) f -> p (t f)", p=P), flatS[:, 0:(WINDOWS + 1) * F]).then_inc(sums_zero, 16)
            for s in range(SLOTS):
                sp.sem_inc(slot_free[s])
            for c in range(CHUNKS):
                sp.wait_ge(records_out[c], 16)
            for p in range(PASSES):
                sp.wait_ge(h_ready, p + 1)
                if p == 3:
                    sp.dma_start(table[p].rearrange("(p t) f -> p (t f)", p=P), flatS[:, 0:WINDOWS * RF]).then_inc(table_out, 16)
                else:
                    sp.dma_start(table[p].rearrange("(p t) f -> p (t f)", p=P), hs[:, 0:WINDOWS * F]).then_inc(table_out, 16)
                with sp.Fori(0, TURNS) as turn:
                    for s in range(SLOTS):
                        g = turn * SLOTS + s
                        sp.wait_ge(slot_free[s], turn + (p * TURNS + 1))
                        sp.dma_start(rec[:, s, :, :].rearrange("p k t -> p (k t)"),
                                     records[:, bass.ds(g * REC, REC)]).then_inc(rec_in[s], 16)
                        if p == TP:
                            sp.dma_start(attrs[:, s, :, :].rearrange("p t j -> p (t j)"),
                                         attr[:, bass.ds(g * (G * R), G * R)]).then_inc(attrs_in[s], 16)
                            sp.dma_start(srcs[:, s, :],
                                         src_flat[bass.ds(g * GE, GE)].partition_broadcast(P)).then_inc(srcs_in[s], 16)
                if p == TP:
                    for half in range(2):
                        if half == 0:
                            sp.wait_ge(sums_scattered, 1)
                        else:
                            sp.wait_ge(sums_read, 1)
                        for i in range(G // 2):
                            sp.dma_start(flatS[:, i * WINDOWS * F:(i + 1) * WINDOWS * F],
                                         sums[half * (G // 2) + i][0:NPAD, :].rearrange("(p t) f -> p (t f)", p=P)
                                         ).then_inc(sums_in[half], 16)
            sp.wait_ge(out_ready, 1)
            sp.dma_start(out[0:(WINDOWS - 1) * P, :].rearrange("(w p) f -> p w f", p=P), xs[:, 0:WINDOWS - 1, :]).then_inc(out_done, 16)
            sp.dma_start(out[(WINDOWS - 1) * P:NODES, :], xs[0:TAIL, WINDOWS - 1, :]).then_inc(out_done, 16)
            sp.wait_ge(out_done, 32)

        @block.gpsimd
        def _(pool):
            pool.iota(iota_n[:, :], [[1, P]], base=0, channel_multiplier=0, allow_small_or_imprecise_dtypes=True).then_inc(iotas, 1)
            pool.iota(iota_r[:, :], [[1, R]], base=0, channel_multiplier=0, allow_small_or_imprecise_dtypes=True).then_inc(iotas, 1)
            pool.iota(start_of[:, :], [[P, WINDOWS]], base=0, channel_multiplier=0, allow_small_or_imprecise_dtypes=True).then_inc(iotas, 1)
            pool.iota(spare[:, :], [[1, 1]], base=NPAD, channel_multiplier=1, allow_small_or_imprecise_dtypes=True).then_inc(iotas, 1)
            pool.memset(ident[:, :], 0.0).then_inc(iotas, 1)
            pool.memset(before[:, :], 1.0).then_inc(iotas, 1)
            pool.wait_ge(iotas, 6)
            pool.affine_select(out=ident[:, :], in_=ident[:, :], compare_op=ALU.not_equal, fill=1.0, base=0,
                               pattern=[[-1, P]], channel_multiplier=1).then_inc(iotas, 1)
            pool.affine_select(out=before[:, :], in_=before[:, :], compare_op=ALU.is_gt, fill=0.0, base=0,
                               pattern=[[-1, P]], channel_multiplier=1).then_inc(iotas, 1)
            pool.wait_ge(ext_ready, 1)
            pool.partition_all_reduce(extr[:, :, :].rearrange("p a g -> p (a g)"), ext[:, :, :].rearrange("p a g -> p (a g)"),
                                      P, bass.bass_isa.ReduceOp.max).then_inc(extr_ready, 1)

            def gather(p, s, turn):
                pool.wait_ge(rec_in[s], turn * 16 + 16 * (p * TURNS + 1))
                pool.wait_ge(expanded_ready[s], turn + (p * TURNS + 1))
                pool.sem_inc(groups_begun)
                field = {3: TYPE_ROW, TP: DST_ROW}.get(p, SRC_ROW)
                for t in range(G):
                    pool.indirect_dma_start(out=rows[:, s, t, :], out_offset=None, in_=table[p],
                                            in_offset=bass.IndirectOffsetOnAxis(ap=rec[:, s, field, t:t + 1], axis=0)
                                            ).then_inc(rows_in[p // 3][s], 16)

            def scatter(s, turn):
                pool.wait_ge(summed_ready[s], turn + 1)
                pool.sem_inc(groups_begun)
                for t in range(G):
                    pool.indirect_dma_start(out=sums[t], out_offset=bass.IndirectOffsetOnAxis(ap=scat[:, s, t:t + 1], axis=0),
                                            in_=summed[:, s, t * F:(t + 1) * F], in_offset=None,
                                            compute_op=ALU.add).then_inc(scattered[s], 16)

            def scatter_landed(s, turn):
                pool.wait_ge(scattered[s], turn * LANDED + LANDED)
                pool.sem_inc(scatter_free[s])

            for s in range(SLOTS):
                pool.sem_inc(expanded_ready[s])
                pool.sem_inc(scatter_free[s])
            for p in range(PASSES):
                pool.wait_ge(table_out, 16 * (p + 1))
                if p != TP:
                    with pool.Fori(0, TURNS) as turn:
                        for s in range(SLOTS):
                            gather(p, s, turn)
                    continue
                pool.wait_ge(sums_zero, 16 * G)
                gather(p, 0, 0)
                gather(p, 1, 0)
                with pool.Fori(0, TURNS - 1) as turn:
                    for s in range(SLOTS):
                        scatter(s, turn)
                        gather(p, (s + 2) % SLOTS, turn + (s + 2) // SLOTS)
                        scatter_landed(s, turn)
                for s in range(SLOTS):
                    scatter(s, TURNS - 1)
                    if s + 2 < SLOTS:
                        gather(p, s + 2, TURNS - 1)
                    scatter_landed(s, TURNS - 1)
                pool.sem_inc(sums_scattered)

        @block.scalar
        def _(act):
            asked = [0]

            def func(out_, in_, f, scale=1.0):
                asked[0] += 1
                act.wait_ge(act_asked, asked[0])
                act.activation(out_, in_, f, scale=scale).then_inc(act_done, 1)

            def stage(n, ka, kb):
                with act.Fori(0, BATCHES) as b:
                    act.wait_ge(turned, b + (n * BATCHES + 1))
                    if kb:
                        act.copy(nbt[0:kb, :], psA[0:kb, 1024:1024 + NB * P])
                    act.copy(nat[0:ka, :], psA[0:ka, 0:NB * P]).then_inc(turned_out, 1)

            act_norm = lambda: func(stat[:, 1, :], stat[:, 1, :], ACT.Sqrt)
            act_norm()
            stage(0, RF, F)
            stage(1, RF, F)
            func(ta[:, 0:WINDOWS * F], tb[:, :], ACT.Exp)
            func(stat[:, 1, :], stat[:, 0, :], ACT.Ln)
            act_norm()
            stage(2, RF, F)
            stage(3, 2 * F, 0)
            stage(4, 2 * F, 0)
            act_norm()
            with act.Fori(0, TURNS) as turn:
                for s in range(SLOTS):
                    act.wait_ge(outer_turned, turn * SLOTS + s + 1)
                    act.copy(outerT, psA[:, :]).then_inc(outer_out, 1)
                    act.wait_ge(msg_product, turn * SLOTS + s + 1)
                    act.activation(msg[:, s % 2, :], psB[:, 0:G * F], ACT.Silu, scale=float(RF) ** -0.5).then_inc(msg_ready, 1)
            stage(5, F, 0)
            stage(6, RF, 0)
            stage(7, RF, 0)
            func(tb[:, :], tb[:, :], ACT.Silu, float(F * F) ** -0.5)
            stage(8, F, 0)
            act_norm()
            stage(9, RF, 0)
            stage(10, F, F)
            gates = flatS[:, 0:WINDOWS * 4 * F].rearrange("p (w k) -> p w k", k=4 * F)
            func(gates[:, :, 0:2 * F], gates[:, :, 0:2 * F], ACT.Sigmoid)
            func(gates[:, :, 2 * F:3 * F], gates[:, :, 2 * F:3 * F], ACT.Tanh)

        @block.tensor
        def _(pe):
            pe.wait_ge(constants_in, n_constants)
            pe.wait_ge(iotas, 8)
            pe.wait_ge(spans_ready, 1)

            def conv(p):
                width = SW if p == 0 else RF

                def pair(k, s):
                    pe.wait_ge(onehot_ready[p], k + 1)
                    for t in range(G):
                        mm = pe.matmul(psC[:, 0:width], onehot[:, t, :], expanded[:, s % 2, t, 0:width],
                                       start=(t == 0), stop=(t == G - 1))
                    mm.then_inc(pair_done[p], 1)

                with pe.Fori(0, TURNS) as turn:
                    for s in range(SLOTS):
                        g = turn * SLOTS + s
                        pe.wait_ge(expanded_ready[s], turn + (p * TURNS + 2))
                        more = pe.value_load(spans[0:1, bass.ds(g, 1), 1], min_val=0, max_val=WINDOWS - 1)
                        k0 = pe.value_load(spans[0:1, bass.ds(g, 1), 2], min_val=0, max_val=GROUPS * WINDOWS)
                        pair(k0, s)
                        with pe.If(more > 0):
                            with pe.Fori(1, more + 1) as i:
                                pair(k0 + i, s)

            def stage(n, ka, wa, kb=0, wb=None, cols=F):
                st = 128 if cols > 64 else 64
                with pe.Fori(0, BATCHES) as b:
                    pe.wait_ge(operands_ready, b + (n * BATCHES + 1))
                    for j in range(NB):
                        if kb:
                            pe.transpose(psA[0:kb, 1024 + j * P:1024 + (j + 1) * P], nb[:, j * kb:(j + 1) * kb], ident[:, :])
                        mm = pe.transpose(psA[0:ka, j * P:(j + 1) * P], na[:, j * ka:(j + 1) * ka], ident[:, :])
                    mm.then_inc(turned, 1)
                    pe.wait_ge(turned_out, b + (n * BATCHES + 1))
                    for j in range(NB):
                        mm = pe.matmul(psB[:, j * st:j * st + cols], nat[0:ka, j * P:(j + 1) * P], W(wa), start=True, stop=not kb)
                        if kb:
                            mm = pe.matmul(psB[:, j * st:j * st + cols], nbt[0:kb, j * P:(j + 1) * P], W(wb), start=False, stop=True)
                    mm.then_inc(product_done, 1)

            conv(0)
            stage(0, RF, "a1", F, "ar1")
            conv(1)
            stage(1, RF, "a2", F, "ar2")
            conv(2)
            stage(2, RF, "b1", F, "br1", cols=2 * F)
            stage(3, 2 * F, "br2")
            stage(4, 2 * F, "b2", cols=RF)
            conv(3)
            with pe.Fori(0, TURNS) as turn:
                for s in range(SLOTS):
                    pe.wait_ge(expanded_ready[s], turn + (TP * TURNS + 2))
                    outer = expanded[:, s % 2, :, :].rearrange("p t k -> p (t k)")[:, 0:GE]
                    for t in range(G):
                        mm = pe.transpose(psA[:, t * P:(t + 1) * P], outer[:, t * P:(t + 1) * P], ident[:, :])
                    mm.then_inc(outer_turned, 1)
                    pe.wait_ge(outer_out, turn * SLOTS + s + 1)
                    for t in range(G):
                        mm = pe.matmul(psB[:, t * F:(t + 1) * F], outerT[:, t * P:(t + 1) * P], W("mtp"), start=True, stop=True)
                    mm.then_inc(msg_product, 1)
                    pe.wait_ge(msg_ready, turn * SLOTS + s + 1)
                    pe.wait_ge(same_ready, turn * SLOTS + s + 1)
                    for t in range(G):
                        mm = pe.matmul(psC[:, t * F:(t + 1) * F], onehot[:, t, :], msg[:, s % 2, t * F:(t + 1) * F], start=True, stop=True)
                    mm.then_inc(same_summed, 1)
            stage(5, F, "mlin")
            stage(6, RF, "utp0")
            stage(7, RF, "utp1")
            stage(8, F, "ulin")
            conv(5)
            stage(9, RF, "emb")
            stage(10, F, "gi", F, "gh", cols=4 * F)

        @block.vector
        def _(dve):
            steps, asked = [0], [0]

            def step(ins):
                steps[0] += 1
                ins.then_inc(dve_steps, 1)
                dve.wait_ge(dve_steps, steps[0])

            def ask(ins):
                asked[0] += 1
                ins.then_inc(act_asked, 1)
                dve.wait_ge(act_done, asked[0])

            def over(ap, n):
                return ap.unsqueeze(2).to_broadcast([P, ap.shape[1], n])

            def cols(t, k):
                return t[:, 0:WINDOWS * k].rearrange("p (w k) -> p w k", k=k)

            x3 = xs[:, :, :]
            h3, h32 = cols(hs, F), cols(hs, 2 * F)
            t3, t32 = cols(ta, F), cols(ta, 2 * F)
            u3 = cols(tb, F)
            S4 = S[:, :, 0:RF].rearrange("p w (r f) -> p w r f", r=R)

            def layernorm():
                step(dve.tensor_reduce(stat[:, 0, :], x3, AX.X, ALU.add))
                step(dve.tensor_scalar(stat[:, 0, :], stat[:, 0, :], 1.0 / F, None, ALU.mult))
                step(dve.tensor_tensor(t3, x3, over(stat[:, 0, :], F), ALU.subtract))
                step(dve.tensor_tensor(u3, t3, t3, ALU.mult))
                step(dve.tensor_reduce(stat[:, 1, :], u3, AX.X, ALU.add))
                ask(dve.tensor_scalar(stat[:, 1, :], stat[:, 1, :], 1.0 / F, EPS, ALU.mult, ALU.add))
                step(dve.reciprocal(stat[:, 0, :], stat[:, 1, :]))
                step(dve.tensor_tensor(t3, t3, over(stat[:, 0, :], F), ALU.mult))
                dve.tensor_scalar(h3, t3, 0.0, None, ALU.max).then_inc(h_ready, 1)

            def clear_sums():
                step(dve.memset(flatS, 0.0))

            def expand(p, s, turn):
                dve.wait_ge(rows_in[p // 3][s], turn * LANDED + LANDED * (p % 3 * TURNS + 1))
                dve.tensor_tensor(expanded[:, s % 2, :, RF:SW], over(rec[:, s, TYPE, :], R),
                                  iota_r[:, :].unsqueeze(1).to_broadcast([P, G, R]), ALU.is_equal).then_inc(masks_ready, 1)
                dve.wait_ge(masks_ready, turn * SLOTS + (CONV.index(p) * GROUPS + s + 1))
                dve.tensor_tensor(expanded[:, s % 2, :, 0:RF].rearrange("p t (r f) -> p t r f", r=R),
                                  rows[:, s, :, :].unsqueeze(2).to_broadcast([P, G, R, F]),
                                  expanded[:, s % 2, :, RF:SW].unsqueeze(3).to_broadcast([P, G, R, F]),
                                  ALU.mult).then_inc(expanded_ready[s], 1)

            def window(p, s, win, k):
                dve.tensor_scalar(rel[:, :], rec[:, s, DST, :], start_of[:, bass.ds(win, 1)], None,
                                  ALU.subtract).then_inc(rel_ready[p], 1)
                dve.wait_ge(rel_ready[p], k + 1)
                dve.tensor_tensor(onehot[:, :, :], iota_n[:, :].unsqueeze(1).to_broadcast([P, G, P]), over(rel[:, :], P),
                                  ALU.is_equal).then_inc(onehot_ready[p], 1)

            def add_window(p, win, k):
                width = SW if p == 0 else RF
                dve.wait_ge(pair_done[p], k + 1)
                at = S[:, bass.ds(win, 1), 0:width].rearrange("p a b -> p (a b)")
                dve.tensor_tensor(at, at, psC[:, 0:width], ALU.add)

            def conv(p):
                def group(s, turn, last=False):
                    g = turn * SLOTS + s
                    lo = dve.value_load(spans[0:1, bass.ds(g, 1), 0], min_val=0, max_val=WINDOWS - 1)
                    more = dve.value_load(spans[0:1, bass.ds(g, 1), 1], min_val=0, max_val=WINDOWS - 1)
                    k0 = dve.value_load(spans[0:1, bass.ds(g, 1), 2], min_val=0, max_val=GROUPS * WINDOWS)
                    window(p, s, lo, k0)
                    if not last:
                        expand(p, (s + 1) % SLOTS, turn + (s + 1) // SLOTS)
                    add_window(p, lo, k0)
                    with dve.If(more > 0):
                        with dve.Fori(1, more + 1) as i:
                            win = within(lo + i, WINDOWS - 1)
                            window(p, s, win, k0 + i)
                            add_window(p, win, k0 + i)
                    dve.sem_inc(slot_free[s])

                expand(p, 0, 0)
                with dve.Fori(0, TURNS - 1) as turn:
                    for s in range(SLOTS):
                        group(s, turn)
                for s in range(SLOTS):
                    group(s, TURNS - 1, last=s == SLOTS - 1)

            def stage(n, load_a, load_b, store, width):
                st = 128 if width > 64 else 64
                with dve.Fori(0, BATCHES) as b:
                    w0 = b * NB
                    if load_b:
                        load_b(w0)
                    load_a(w0).then_inc(operands_ready, 1)
                    dve.wait_ge(product_done, b + (n * BATCHES + 1))
                    store(w0, psB[:, 0:NB * st].rearrange("p (w k) -> p w k", k=st)[:, :, 0:width])

            def batch(t, w0):
                return t[:, bass.ds(w0, NB), :]

            def from_sums(w0):
                return dve.tensor_tensor(na[:, :].rearrange("p (w r f) -> p w r f", w=NB, r=R), S4[:, bass.ds(w0, NB), :, :],
                                         batch(inv, w0).unsqueeze(3).to_broadcast([P, NB, R, F]), ALU.mult)

            def from_plain_sums(w0):
                return dve.tensor_copy(na[:, :].rearrange("p (w k) -> p w k", w=NB), S[:, bass.ds(w0, NB), 0:RF])

            def from_tile(t, k, to=na):
                return lambda w0: dve.tensor_copy(to[:, 0:NB * k].rearrange("p (w k) -> p w k", w=NB), batch(t, w0))

            def plus(t, k, bias):
                return lambda w0, psum: dve.tensor_tensor(batch(t, w0), psum, bias.unsqueeze(1).to_broadcast([P, NB, k]), ALU.add)

            def times(t, scale):
                return lambda w0, psum: dve.tensor_scalar(batch(t, w0), psum, scale, None, ALU.mult)

            def settle():
                step(dve.tensor_copy(rel[:, 0:1], spare[:, :]))

            dve.memset(xs[:, WINDOWS - 1, :], 0.0).then_inc(cleared, 1)
            dve.memset(wt[:, WP["gi"][0]:WP["gh"][0] + 4 * F], 0.0).then_inc(cleared, 1)
            dve.memset(span[:, 3, :], 1.0)

            dve.wait_ge(iotas, 8)
            for c in range(CHUNKS):
                dve.wait_ge(edges_in[c], 48)
                e = edge_chunk(c)
                r = record_chunk(c)
                if c >= 2:
                    dve.wait_ge(records_out[c - 2], 16)
                ev = e.rearrange("p k (g t) -> p k g t", t=G)
                for node, field, hi in ((0, SRC_ROW, TYPE_ROW), (1, DST_ROW, SRC)):
                    dve.tensor_scalar(r[:, :, field, :], ev[:, node], P - 1, None, ALU.bitwise_and)
                    step(dve.tensor_scalar(r[:, :, hi, :], ev[:, node], 7, None, ALU.logical_shift_right))
                    if node == 1:
                        step(dve.tensor_reduce(ext[:, 0, c * CG:(c + 1) * CG], r[:, :, hi, :], AX.X, ALU.max))
                        step(dve.tensor_reduce(ext[:, 1, c * CG:(c + 1) * CG], r[:, :, hi, :], AX.X, ALU.min))
                    step(dve.scalar_tensor_tensor(out=r[:, :, field, :], in0=r[:, :, field, :], scalar=float(WINDOWS),
                                                  in1=r[:, :, hi, :], op0=ALU.mult, op1=ALU.add))
                dve.scalar_tensor_tensor(out=r[:, :, TYPE_ROW, :], in0=r[:, :, SRC_ROW, :], scalar=float(R),
                                         in1=ev[:, 2], op0=ALU.mult, op1=ALU.add)
                dve.tensor_copy(r[:, :, DST, :], ev[:, 1])
                dve.tensor_copy(r[:, :, TYPE, :], ev[:, 2])
                dve.tensor_copy(r[:, :, SRC, :], ev[:, 0]).then_inc(records_built, 1)
            step(dve.tensor_scalar(ext[:, 1, :], ext[:, 1, :], -1.0, None, ALU.mult))
            dve.tensor_copy(rel[:, 0:1], spare[:, :]).then_inc(ext_ready, 1)
            for c in range(CHUNKS):
                dve.wait_ge(records_out[c], 16)
            dve.memset(flatS, 0.0).then_inc(cleared, 1)

            dve.wait_ge(extr_ready, 1)
            step(dve.tensor_scalar(span[:, 0, :], extr[0:1, 1, :], -1.0, None, ALU.mult))
            step(dve.tensor_tensor(span[:, 1, :], extr[0:1, 0, :], span[:, 0, :], ALU.subtract))
            step(dve.tensor_scalar(span[:, 4, :], span[:, 1, :], 1.0, None, ALU.add))
            step(dve.tensor_tensor_scan(span[:, 5, :], span[:, 3, :], span[:, 4, :], 0.0, ALU.mult, ALU.add))
            step(dve.tensor_tensor(span[:, 2, :], span[:, 5, :], span[:, 4, :], ALU.subtract))
            dve.tensor_copy(spans[:, :, 0], span[:, 0, :])
            dve.tensor_copy(spans[:, :, 1], span[:, 1, :])
            dve.tensor_copy(spans[:, :, 2], span[:, 2, :]).then_inc(spans_ready, 1)
            dve.wait_ge(spans_ready, 1)

            dve.wait_ge(x_in, 32)
            layernorm()
            dve.wait_ge(sums_zero, 16 * G)

            conv(0)
            settle()
            step(dve.tensor_scalar(inv[:, :, :], S[:, :, RF:SW], 1.0, None, ALU.max))
            step(dve.reciprocal(inv[:, :, :], inv[:, :, :]))
            dve.wait_ge(constants_in, n_constants)
            stage(0, from_sums, from_tile(h3, F, nb), plus(t3, F, B("ab1")), F)
            settle()
            dve.tensor_scalar(h3, t3, 0.0, None, ALU.max).then_inc(h_ready, 1)
            clear_sums()
            conv(1)
            settle()
            stage(1, from_sums, from_tile(h3, F, nb), plus(t3, F, B("ab2")), F)
            settle()
            step(dve.tensor_reduce(stat[:, 0, :], t3, AX.X, ALU.max))
            step(dve.tensor_tensor(u3, t3, over(stat[:, 0, :], F), ALU.subtract))
            step(dve.tensor_tensor(x3, x3, u3, ALU.add))
            ask(dve.tensor_copy(rel[:, 0:1], spare[:, :]))
            ask(dve.tensor_reduce(stat[:, 0, :], t3, AX.X, ALU.add))
            step(dve.tensor_tensor(x3, x3, over(stat[:, 1, :], F), ALU.subtract))
            layernorm()

            clear_sums()
            conv(2)
            settle()
            stage(2, from_sums, from_tile(h3, F, nb), plus(t32, 2 * F, B("bb1")), 2 * F)
            settle()
            step(dve.tensor_scalar(h32, t32, 0.0, None, ALU.max))
            stage(3, from_tile(h32, 2 * F), None, plus(u3, F, B("bb2")), F)
            Y = flatS[:, 0:WINDOWS * RF].rearrange("p (w k) -> p w k", k=RF)
            stage(4, from_tile(h32, 2 * F), None, lambda w0, psum: dve.tensor_copy(batch(Y, w0), psum), RF)
            dve.tensor_copy(rel[:, 0:1], spare[:, :]).then_inc(h_ready, 1)
            step(dve.tensor_tensor(x3, x3, u3, ALU.add))
            dve.wait_ge(table_out, 16 * 4)
            clear_sums()
            conv(3)
            settle()
            step(dve.tensor_tensor(S4, S4, inv[:, :, :].unsqueeze(3).to_broadcast([P, WINDOWS, R, F]), ALU.mult))
            for r in range(R):
                step(dve.tensor_tensor(x3, x3, S4[:, :, r, :], ALU.add))
            layernorm()

            with dve.Fori(0, TURNS) as turn:
                for s in range(SLOTS):
                    k = turn * SLOTS + s
                    dve.wait_ge(rows_in[TP // 3][s], turn * LANDED + LANDED * (TP % 3 * TURNS + 1))
                    dve.wait_ge(attrs_in[s], turn * 16 + 16)
                    outer = expanded[:, s % 2, :, :].rearrange("p t k -> p (t k)")[:, 0:GE]
                    dve.tensor_tensor(outer.rearrange("p (t j f) -> p t j f", t=G, j=R),
                                      rows[:, s, :, :].unsqueeze(2).to_broadcast([P, G, R, F]),
                                      attrs[:, s, :, :].unsqueeze(3).to_broadcast([P, G, R, F]),
                                      ALU.mult).then_inc(expanded_ready[s], 1)
                    dve.wait_ge(srcs_in[s], turn * 16 + 16)
                    dve.tensor_tensor(onehot[:, :, :], srcs[:, s, :].rearrange("p (t e) -> p t e", t=G),
                                      over(rec[:, s, SRC, :], P), ALU.is_equal).then_inc(same_ready, 1)
                    dve.wait_ge(same_ready, k + 1)
                    dve.tensor_tensor(earlier, onehot[:, :, :], before[:, :].unsqueeze(1).to_broadcast([P, G, P]),
                                      ALU.mult).then_inc(dup_steps, 1)
                    dve.wait_ge(dup_steps, k * 4 + 1)
                    dve.tensor_reduce(dup[:, 0, :], earlier, AX.X, ALU.add)
                    dve.tensor_scalar(dup[:, 1, :], rec[:, s, SRC_ROW, :], spare[:, 0:1], -1.0, ALU.subtract,
                                      ALU.mult).then_inc(dup_steps, 1)
                    dve.wait_ge(dup_steps, k * 4 + 2)
                    dve.scalar_tensor_tensor(out=dup[:, 2, :], in0=dup[:, 0, :], scalar=0.0, in1=dup[:, 1, :],
                                             op0=ALU.is_gt, op1=ALU.mult).then_inc(dup_steps, 1)
                    dve.wait_ge(dup_steps, k * 4 + 3)
                    dve.wait_ge(scatter_free[s], turn + 1)
                    dve.tensor_tensor(scat[:, s, :], dup[:, 2, :], rec[:, s, SRC_ROW, :], ALU.add).then_inc(dup_steps, 1)
                    dve.wait_ge(dup_steps, k * 4 + 4)
                    dve.sem_inc(slot_free[s])
                    dve.wait_ge(same_summed, k + 1)
                    dve.tensor_copy(summed[:, s, :], psC[:, 0:G * F]).then_inc(summed_ready[s], 1)
            T8 = flatS[:, 0:(G // 2) * WINDOWS * F].rearrange("p (i k) -> p i k", i=G // 2)
            for half in range(2):
                dve.wait_ge(sums_in[half], 16 * (G // 2))
                for i in range(G // 2):
                    if half == 0 and i == 0:
                        step(dve.tensor_copy(tb[:, :], T8[:, 0, :]))
                    else:
                        step(dve.tensor_tensor(tb[:, :], tb[:, :], T8[:, i, :], ALU.add))
                if half == 0:
                    dve.sem_inc(sums_read)
            stage(5, from_tile(u3, F), None, times(t3, float(F) ** -0.5), F)
            settle()
            Z = flatS[:, 0:WINDOWS * RF].rearrange("p (w i f) -> p w i f", i=R, f=F)
            Z3 = flatS[:, 0:WINDOWS * RF].rearrange("p (w k) -> p w k", k=RF)
            v3 = cols(hs[:, WINDOWS * F:], F)
            for half in range(2):
                step(dve.tensor_tensor(Z, h3[:, :, half * R:(half + 1) * R].unsqueeze(3).to_broadcast([P, WINDOWS, R, F]),
                                       t3.unsqueeze(2).to_broadcast([P, WINDOWS, R, F]), ALU.mult))
                to = (u3, v3)[half]
                stage(6 + half, from_tile(Z3, RF), None, lambda w0, psum, to=to: dve.tensor_copy(batch(to, w0), psum), F)
                settle()
            ask(dve.tensor_tensor(u3, u3, v3, ALU.add))
            stage(8, from_tile(u3, F), None, times(t3, float(F) ** -0.5), F)
            settle()
            step(dve.tensor_tensor(t3, t3, h3, ALU.add))
            step(dve.tensor_tensor(x3, x3, t3, ALU.add))
            layernorm()

            clear_sums()
            dve.tensor_tensor(bg[:, 0:2 * F], B("ih", 0, 2 * F), B("hh", 0, 2 * F), ALU.add)
            dve.tensor_copy(bg[:, 2 * F:3 * F], B("ih", 2 * F))
            step(dve.tensor_copy(bg[:, 3 * F:4 * F], B("hh", 2 * F)))
            conv(5)
            settle()
            stage(9, from_plain_sums, None, times(t3, 1.0), F)
            settle()
            gates = flatS[:, 0:WINDOWS * 4 * F].rearrange("p (w k) -> p w k", k=4 * F)
            stage(10, from_tile(t3, F), from_tile(h3, F, nb), plus(gates, 4 * F, bg[:, :]), 4 * F)
            ask(dve.tensor_copy(rel[:, 0:1], spare[:, :]))
            step(dve.tensor_tensor(t3, gates[:, :, 0:F], gates[:, :, 3 * F:4 * F], ALU.mult))
            ask(dve.tensor_tensor(gates[:, :, 2 * F:3 * F], gates[:, :, 2 * F:3 * F], t3, ALU.add))
            new = gates[:, :, 2 * F:3 * F]
            step(dve.tensor_tensor(t3, h3, new, ALU.subtract))
            step(dve.tensor_tensor(t3, t3, gates[:, :, F:2 * F], ALU.mult))
            step(dve.tensor_tensor(t3, t3, new, ALU.add))
            dve.tensor_tensor(x3, x3, t3, ALU.add).then_inc(out_ready, 1)


def kernel(**inputs):
    import numpy as np
    import concourse.bacc as bacc
    from concourse.bass_utils import run_bass_kernel_spmd

    def edges(name, fill):
        a = np.asarray(inputs[name])
        return np.concatenate([a, np.full((EPAD - EDGES,) + a.shape[1:], fill, a.dtype)])

    def tiles(a):
        return np.ascontiguousarray(a.reshape(EC, P, -1).transpose(1, 0, 2).reshape(P, -1))

    def get(name, shape=None, perm=None):
        a = np.asarray(inputs[name])
        a = a if perm is None else a.transpose(perm)
        return np.ascontiguousarray(a if shape is None else a.reshape(shape))

    none = NPAD - 1
    src = edges("src", none)
    arrays = {
        "x": get("x"), "src": tiles(src), "dst": tiles(edges("dst", none)), "typ": tiles(edges("edge_type_8", 0)),
        "src_flat": src, "attr": tiles(edges("edge_attr_8", 0)),
        "a1": get("L0_gnn_W1", (RF, F)), "ar1": get("L0_gnn_root1"), "a2": get("L0_gnn_W2", (RF, F)), "ar2": get("L0_gnn_root2"),
        "b1": get("L1_gnn_W1", (RF, 2 * F)), "br1": get("L1_gnn_root1"),
        "b2": get("L1_gnn_W2", (2 * F, RF), (1, 0, 2)), "br2": get("L1_gnn_root2"),
        "mtp": get("L2_gnn_W_msg_tp", (RF, F), (1, 0, 2)), "mlin": get("L2_gnn_W_msg_lin"),
        "utp0": get("L2_gnn_W_upd_tp", (F * F, F))[0:RF], "utp1": get("L2_gnn_W_upd_tp", (F * F, F))[RF:],
        "ulin": get("L2_gnn_W_upd_lin"),
        "emb": np.ascontiguousarray(get("L3_gnn_edge_emb", (R, F, F)).transpose(0, 2, 1).reshape(RF, F)),
        "gi": get("L3_gnn_w_ih", None, (1, 0)), "gh": get("L3_gnn_w_hh", None, (1, 0)),
        "ab1": get("L0_gnn_b1"), "ab2": get("L0_gnn_b2"), "bb1": get("L1_gnn_b1"), "bb2": get("L1_gnn_b2"),
        "ih": get("L3_gnn_b_ih"), "hh": get("L3_gnn_b_hh"),
    }
    nc = bacc.Bacc("TRN2", target_bir_lowering=False, num_devices=1)
    d = {n: nc.dram_tensor(f"in_{n}", a.shape, mybir.dt.from_np(a.dtype), kind="ExternalInput").ap() for n, a in arrays.items()}
    out = nc.dram_tensor("out_x", (NODES, F), F32, kind="ExternalOutput").ap()
    gnn_kernel(nc, *(d[n] for n in ("x", "src", "dst", "typ", "src_flat", "attr")),
               {n: d[n] for n, *_ in WEIGHTS}, {n: d[n] for n, _ in BIASES}, out)
    r = run_bass_kernel_spmd(nc, [{f"in_{n}": a for n, a in arrays.items()}], core_ids=[0])
    return r.results[0]["out_x"]
```

```python
from contextlib import ExitStack

import concourse.bass as bass
from concourse import mybir

F32 = mybir.dt.float32
BF16 = mybir.dt.bfloat16
I32 = mybir.dt.int32
I16 = mybir.dt.int16
ALU = mybir.AluOpType
ACT = mybir.ActivationFunctionType
AX = mybir.AxisListType

P = 128
NODES = 12500
EDGES = 400000
F = 16
R = 8
WINDOWS = -(-NODES // P)
NPAD = WINDOWS * P
TAIL = NODES - (WINDOWS - 1) * P
G = 16
GE = G * P
SLOTS = 4
TURNS = -(-EDGES // (GE * SLOTS))
GROUPS = TURNS * SLOTS
EPAD = GROUPS * GE
EC = EPAD // P
FIELDS = 6
SRC_ROW, TYPE_ROW, DST, TYPE, SRC, BLOCK = range(FIELDS)
REC = FIELDS * G
CHUNKS = 4
CG = GROUPS // CHUNKS
RF = R * F
SW = RF + R
NB = 7
BATCHES = WINDOWS // NB
OWN = 4
WAYS = 8
BLOCKS = -(-WINDOWS // WAYS)
HALF = G // 2
PARTS = 3
EPS = 1e-5
PASSES = 6
CONV = [0, 1, 2, 3, 5]
TP = 4
BY_TYPE = 3


def own(p):
    return 0 if p == BY_TYPE else OWN


def landed(p):
    return 16 * (G - own(p))


def landed_before(p):
    i = CONV.index(p)
    return sum(landed(q) for q in CONV[i - i % 3:i]) * TURNS


WEIGHTS = [("a1", 128, 16), ("ar1", 16, 16), ("a2", 128, 16), ("ar2", 16, 16), ("b1", 128, 32), ("br1", 16, 32),
           ("b2", 32, 128), ("br2", 32, 16), ("mtp", 128, 16), ("mlin", 16, 16), ("utp0", 128, 16), ("utp1", 128, 16),
           ("ulin", 16, 16), ("emb", 128, 16), ("gi", 16, 64), ("gh", 16, 64)]
BIASES = [("ab1", 16), ("ab2", 16), ("bb1", 32), ("bb2", 16), ("ih", 48), ("hh", 48)]


def places(list_of_sizes):
    at, found = 0, {}
    for name, *_, n in list_of_sizes:
        found[name] = (at, n)
        at += n
    return found, at


def gnn_kernel(nc, x, src, dst, typ, src_flat, dst_flat, attr, w, biases, out):
    WP, WCOLS = places(WEIGHTS)
    BP, BCOLS = places(BIASES)
    with ExitStack() as ctx:
        def sb(name, shape, dt=F32):
            return ctx.enter_context(nc.sbuf_tensor(name, shape, dt))

        def ps(name, shape):
            return ctx.enter_context(nc.psum_tensor(name, shape, F32))

        def sem(name):
            return ctx.enter_context(nc.semaphore(name))

        def sems(name, n):
            return [sem(f"{name}{i}") for i in range(n)]

        table = {p: nc.dram_tensor(f"table{p}", (NPAD, F), F32, kind="Internal").ap() for p in CONV if p != 3}
        table[3] = nc.dram_tensor("table3", (NPAD * R, F), F32, kind="Internal").ap()
        place_flat = nc.dram_tensor("place_flat", (EPAD,), I16, kind="Internal").ap()
        records = nc.dram_tensor("records", (P, GROUPS * REC), I32, kind="Internal").ap()
        sums = [nc.dram_tensor(f"sums{i}", (NPAD + P, F), F32, kind="Internal").ap() for i in range(G)]

        xs = sb("xs", [P, WINDOWS, F])
        hs = sb("hs", [P, WINDOWS * 2 * F])
        S = sb("S", [P, WINDOWS + 1, SW])
        ta = sb("ta", [P, WINDOWS * 2 * F])
        tb = sb("tb", [P, WINDOWS * F])
        inv = sb("inv", [P, WINDOWS, R])
        stat = sb("stat", [P, 2, WINDOWS])
        rec = sb("rec", [P, SLOTS, FIELDS, G], I32)
        rows = sb("rows", [P, SLOTS, G, F])
        expanded = sb("expanded", [P, 2, G, SW])
        onehot = sb("onehot", [P, G, P])
        frame = sb("frame", [P, P])
        wraps = sb("wraps", [P, P])
        none = sb("none", [P, 1])
        iota_n = sb("iota_n", [P, P])
        iota_r = sb("iota_r", [P, R])
        ident = sb("ident", [P, P])
        before = sb("before", [P, P], BF16)
        hparts = sb("hparts", [P, BLOCKS * WAYS, PARTS, F], BF16)
        msg_parts = sb("msg_parts", [P, PARTS, G * F], BF16)
        msg_rest = sb("msg_rest", [P, G * F])
        place = sb("place", [P, SLOTS, OWN * P], I16)
        fine = sb("fine", [P, 2, WAYS, OWN * P], BF16)
        block_of = sb("block_of", [P, OWN, BLOCKS])
        picked = sb("picked", [P, OWN, BLOCKS, F])
        spare = sb("spare", [P, 1])
        node_of = sb("node_of", [P, WINDOWS])
        wt = sb("wt", [P, WCOLS])
        bt = sb("bt", [P, BCOLS])
        bg = sb("bg", [P, 4 * F])
        na = sb("na", [P, NB * P])
        nb = sb("nb", [P, NB * 2 * F])
        nat = sb("nat", [P, NB * P])
        nbt = sb("nbt", [P, NB * P])
        ext = sb("ext", [P, 2, GROUPS])
        extr = sb("extr", [P, 2, GROUPS])
        lowest = sb("lowest", [P, GROUPS], I32)
        low_place = sb("low_place", [P, GROUPS])
        low_window = sb("low_window", [P, GROUPS])
        kept = sb("kept", [P, GROUPS])
        wrapped = sb("wrapped", [P, GROUPS])
        span = sb("span", [1, 4, GROUPS])
        span_of = sb("span_of", [1, 3, GROUPS], I32)
        spans = sb("spans", [1, GROUPS, 5], I32)
        attrs = sb("attrs", [P, SLOTS, G, R])
        msg = sb("msg", [P, 2, G * F])
        summed = sb("summed", [P, SLOTS, G * F])
        scat = sb("scat", [P, SLOTS, G], I32)
        dup = sb("dup", [P, 3, G])

        psA = ps("psA", [P, 2048])
        psB = ps("psB", [P, 1536])
        psC = ps("psC", [P, 512])

        flatS = S[:, :, :].rearrange("p w f -> p (w f)")
        wide = flatS[:, 0:4 * GE].bitcast(I32).rearrange("p (b k e) -> p b k e", b=2, k=2)
        outerT = flatS[:, 4 * GE:5 * GE]
        earlier = flatS[:, 5 * GE:5 * GE + GE // 2].bitcast(BF16).rearrange("p (t e) -> p t e", t=G)
        outer = expanded[:, 0, :, :].rearrange("p t k -> p (t k)")[:, 0:GE]
        target = expanded[:, 1, :, :].rearrange("p t k -> p (t k)")[:, 0:GE // 2].bitcast(BF16)
        extra_target = ta[:, 0:GE // 2].bitcast(BF16)
        same = onehot[:, :, :].rearrange("p t e -> p (t e)")[:, 0:GE // 2].bitcast(BF16).rearrange("p (t e) -> p t e", t=G)
        block_parts = hparts[:, :, :, :].rearrange("p (b w) k f -> p b w k f", w=WAYS)

        def gathered_rows(s, t):
            at = s % 2 * 1024 + t // 2 * 512 + t % 2 * BLOCKS * F
            return psA[:, at:at + BLOCKS * F]

        row_parts = psB[:, 512:1536].rearrange("p (b n) -> p b n", b=2)[:, :, 0:HALF * PARTS * F].rearrange(
            "p b (t k f) -> p b t k f", t=HALF, k=PARTS)

        def W(name):
            rows_of = {n: k for n, k, _ in WEIGHTS}
            at, n = WP[name]
            return wt[0:rows_of[name], at:at + n]

        def B(name, lo=0, hi=None):
            at, n = BP[name]
            return bt[:, at + lo:at + (n if hi is None else hi)]

        constants_in = sem("constants_in")
        x_in = sem("x_in")
        iotas = sem("iotas")
        edges_in = sems("edges_in", CHUNKS)
        records_built = sem("records_built")
        records_out = sems("records_out", CHUNKS)
        ext_ready = sem("ext_ready")
        extr_ready = sem("extr_ready")
        spans_ready = sem("spans_ready")
        cleared = sem("cleared")
        sums_zero = sem("sums_zero")
        dve_steps = sem("dve_steps")
        act_asked = sem("act_asked")
        act_done = sem("act_done")
        h_ready = sem("h_ready")
        table_out = sem("table_out")
        slot_free = sems("slot_free", SLOTS)
        rec_in = sems("rec_in", SLOTS)
        rows_in = [sems(f"rows_in_{k}_", SLOTS) for k in range(2)]
        masks_ready = sem("masks_ready")
        groups_begun = sem("groups_begun")
        expanded_ready = sems("expanded_ready", SLOTS)
        first_ready = {p: sem(f"first_ready{p}") for p in CONV}
        first_done = {p: sem(f"first_done{p}") for p in CONV}
        frame_steps = {p: sem(f"frame_steps{p}") for p in CONV}
        more_frames = {p: sem(f"more_frames{p}") for p in CONV}
        more_ready = {p: sem(f"more_ready{p}") for p in CONV}
        more_done = {p: sem(f"more_done{p}") for p in CONV}
        flat_in = sem("flat_in")
        places_built = sem("places_built")
        places_out = sem("places_out")
        place_in = sems("place_in", SLOTS)
        fine_ready = sem("fine_ready")
        own_gathered = sem("own_gathered")
        pick_steps = sem("pick_steps")
        operands_ready = sem("operands_ready")
        turned = sem("turned")
        turned_out = sem("turned_out")
        product_done = sem("product_done")
        batch_done = sem("batch_done")
        attrs_in = sems("attrs_in", SLOTS)
        wide_in = sems("wide_in", 2)
        wide_free = sems("wide_free", 2)
        target_ready = sem("target_ready")
        extra_ready = sem("extra_ready")
        target_used = sem("target_used")
        extra_used = sem("extra_used")
        outer_turned = sem("outer_turned")
        outer_out = sem("outer_out")
        msg_product = sem("msg_product")
        msg_ready = sem("msg_ready")
        parts_ready = sem("parts_ready")
        split_steps = sem("split_steps")
        rows_summed = sem("rows_summed")
        same_ready = sem("same_ready")
        same_summed = sem("same_summed")
        summed_ready = sems("summed_ready", SLOTS)
        scattered = [sems(f"scattered{half}_", SLOTS) for half in range(2)]
        scatter_free = sems("scatter_free", SLOTS)
        dup_steps = sem("dup_steps")
        sums_scattered = sem("sums_scattered")
        sums_in = sems("sums_in", 2)
        sums_read = sem("sums_read")
        out_ready = sem("out_ready")
        out_done = sem("out_done")

        n_constants = 16 * (len(WEIGHTS) + 2 + len(BIASES))

        def hybrid(p):
            return len([q for q in CONV[:CONV.index(p)] if own(q)])

        def within(v, hi):
            return nc.s_assert_within(v, 0, hi, skip_runtime_bounds_check_because="the tables of spans hold windows alone")

        block = ctx.enter_context(nc.Block())

        def edge_chunk(c):
            return flatS[:, 0:3 * CG * G].bitcast(I32).rearrange("p (k e) -> p k e", k=3)

        def record_chunk(c):
            at = 3 * CG * G + (c % 2) * CG * REC
            return flatS[:, at:at + CG * REC].bitcast(I32).rearrange("p (g k t) -> p g k t", g=CG, k=FIELDS)

        def store_records(sp, c):
            sp.wait_ge(records_built, c + 1)
            sp.dma_start(records[:, c * CG * REC:(c + 1) * CG * REC],
                         record_chunk(c).rearrange("p g k t -> p (g k t)")).then_inc(records_out[c], 16)

        @block.sync
        def _(sp):
            sp.dma_start(xs[:, 0:WINDOWS - 1, :], x[0:(WINDOWS - 1) * P, :].rearrange("(w p) f -> p w f", p=P)).then_inc(x_in, 16)
            sp.wait_ge(cleared, 2)
            sp.dma_start(xs[0:TAIL, WINDOWS - 1, :], x[(WINDOWS - 1) * P:NODES, :]).then_inc(x_in, 16)
            sp.dma_start(ta[:, :].bitcast(I32), src_flat.rearrange("(p e) -> p e", p=P)).then_inc(flat_in, 16)
            for c in range(CHUNKS):
                if c:
                    store_records(sp, c - 1)
                for i, a in enumerate((src, dst, typ)):
                    sp.dma_start(edge_chunk(c)[:, i, :], a[:, c * CG * G:(c + 1) * CG * G]).then_inc(edges_in[c], 16)
                if c == 0:
                    for name, k, n in WEIGHTS:
                        if name in ("gi", "gh"):
                            at, _n = WP[name]
                            sp.dma_start(wt[0:F, at:at + 2 * F], w[name][:, 0:2 * F]).then_inc(constants_in, 16)
                            to = at + 2 * F if name == "gi" else at + 3 * F
                            sp.dma_start(wt[0:F, to:to + F], w[name][:, 2 * F:3 * F]).then_inc(constants_in, 16)
                        else:
                            sp.dma_start(W(name), w[name]).then_inc(constants_in, 16)
                    for name, n in BIASES:
                        sp.dma_start(B(name), biases[name].partition_broadcast(P)).then_inc(constants_in, 16)
            store_records(sp, CHUNKS - 1)
            sp.wait_ge(places_built, 1)
            sp.dma_start(place_flat.rearrange("(p e) -> p e", p=P), tb[:, :].bitcast(I16)).then_inc(places_out, 16)
            sp.wait_ge(cleared, 3)
            for i in range(G):
                sp.dma_start(sums[i].rearrange("(p t) f -> p (t f)", p=P), flatS[:, 0:(WINDOWS + 1) * F]).then_inc(sums_zero, 16)
            for s in range(SLOTS):
                sp.sem_inc(slot_free[s])
            for b in range(2):
                sp.sem_inc(wide_free[b])
            for c in range(CHUNKS):
                sp.wait_ge(records_out[c], 16)
            sp.wait_ge(places_out, 16)
            for p in range(PASSES):
                sp.wait_ge(h_ready, p + 1)
                if p == 3:
                    sp.dma_start(table[p].rearrange("(p t) f -> p (t f)", p=P), flatS[:, 0:WINDOWS * RF]).then_inc(table_out, 16)
                elif p != TP:
                    sp.dma_start(table[p].rearrange("(p t) f -> p (t f)", p=P), hs[:, 0:WINDOWS * F]).then_inc(table_out, 16)
                with sp.Fori(0, TURNS) as turn:
                    for s in range(SLOTS):
                        g = turn * SLOTS + s
                        sp.wait_ge(slot_free[s], turn + (p * TURNS + 1))
                        sp.dma_start(rec[:, s, :, :].rearrange("p k t -> p (k t)"),
                                     records[:, bass.ds(g * REC, REC)]).then_inc(rec_in[s], 16)
                        if p in CONV and own(p):
                            sp.dma_start(place[:, s, :], place_flat[bass.ds(g * GE + (G - OWN) * P, OWN * P)].partition_broadcast(P)
                                         ).then_inc(place_in[s], 16)
                        if p == TP:
                            sp.dma_start(attrs[:, s, :, :].rearrange("p t j -> p (t j)"),
                                         attr[:, bass.ds(g * (G * R), G * R)]).then_inc(attrs_in[s], 16)
                            sp.wait_ge(wide_free[s % 2], turn * 2 + (s // 2 + 1))
                            for k, flat in enumerate((src_flat, dst_flat)):
                                sp.dma_start(wide[:, s % 2, k, :],
                                             flat[bass.ds(g * GE, GE)].partition_broadcast(P)).then_inc(wide_in[s % 2], 16)
                if p == TP:
                    for half in range(2):
                        if half == 0:
                            sp.wait_ge(sums_scattered, 1)
                        else:
                            sp.wait_ge(sums_read, 1)
                        for i in range(G // 2):
                            sp.dma_start(flatS[:, i * WINDOWS * F:(i + 1) * WINDOWS * F],
                                         sums[half * (G // 2) + i][0:NPAD, :].rearrange("(p t) f -> p (t f)", p=P)
                                         ).then_inc(sums_in[half], 16)
            sp.wait_ge(out_ready, 1)
            sp.dma_start(out[0:(WINDOWS - 1) * P, :].rearrange("(w p) f -> p w f", p=P), xs[:, 0:WINDOWS - 1, :]).then_inc(out_done, 16)
            sp.dma_start(out[(WINDOWS - 1) * P:NODES, :], xs[0:TAIL, WINDOWS - 1, :]).then_inc(out_done, 16)
            sp.wait_ge(out_done, 32)

        @block.gpsimd
        def _(pool):
            pool.iota(iota_n[:, :], [[1, P]], base=0, channel_multiplier=0, allow_small_or_imprecise_dtypes=True).then_inc(iotas, 1)
            pool.iota(iota_r[:, :], [[1, R]], base=0, channel_multiplier=0, allow_small_or_imprecise_dtypes=True).then_inc(iotas, 1)
            pool.iota(node_of[:, :], [[P, WINDOWS]], base=0, channel_multiplier=1, allow_small_or_imprecise_dtypes=True).then_inc(iotas, 1)
            pool.iota(spare[:, :], [[1, 1]], base=NPAD, channel_multiplier=1, allow_small_or_imprecise_dtypes=True).then_inc(iotas, 1)
            pool.memset(ident[:, :], 0.0).then_inc(iotas, 1)
            pool.memset(before[:, :], 1.0).then_inc(iotas, 1)
            pool.wait_ge(iotas, 6)
            pool.affine_select(out=ident[:, :], in_=ident[:, :], compare_op=ALU.not_equal, fill=1.0, base=0,
                               pattern=[[-1, P]], channel_multiplier=1).then_inc(iotas, 1)
            pool.affine_select(out=before[:, :], in_=before[:, :], compare_op=ALU.is_gt, fill=0.0, base=0,
                               pattern=[[-1, P]], channel_multiplier=1).then_inc(iotas, 1)
            pool.wait_ge(ext_ready, 1)
            pool.partition_all_reduce(extr[:, :, :].rearrange("p a g -> p (a g)"), ext[:, :, :].rearrange("p a g -> p (a g)"),
                                      P, bass.bass_isa.ReduceOp.max).then_inc(extr_ready, 1)

            def gather(p, s, turn):
                pool.wait_ge(rec_in[s], turn * 16 + 16 * (p * TURNS + 1))
                pool.wait_ge(expanded_ready[s], turn + (p * TURNS + 1))
                pool.sem_inc(groups_begun)
                field = TYPE_ROW if p == BY_TYPE else SRC_ROW
                for t in range(G - own(p)):
                    pool.indirect_dma_start(out=rows[:, s, t, :], out_offset=None, in_=table[p],
                                            in_offset=bass.IndirectOffsetOnAxis(ap=rec[:, s, field, t:t + 1], axis=0)
                                            ).then_inc(rows_in[CONV.index(p) // 3][s], 16)

            def scatter(s, turn, half):
                pool.wait_ge(summed_ready[s], turn + 1)
                pool.sem_inc(groups_begun)
                for t in range(half * HALF, (half + 1) * HALF):
                    pool.indirect_dma_start(out=sums[t], out_offset=bass.IndirectOffsetOnAxis(ap=scat[:, s, t:t + 1], axis=0),
                                            in_=summed[:, s, t * F:(t + 1) * F], in_offset=None,
                                            compute_op=ALU.add).then_inc(scattered[half][s], 16)

            def scatter_after(s, turn, last=False):
                for half in range(2):
                    pool.wait_ge(scattered[half][s], turn * (16 * HALF) + 16 * HALF)
                    if half:
                        pool.sem_inc(scatter_free[s])
                    if not last:
                        scatter((s + 1) % SLOTS, turn + (s + 1) // SLOTS, half)

            for s in range(SLOTS):
                pool.sem_inc(expanded_ready[s])
                pool.sem_inc(scatter_free[s])
            for p in range(PASSES):
                if p != TP:
                    pool.wait_ge(table_out, 16 * (CONV.index(p) + 1))
                    with pool.Fori(0, TURNS) as turn:
                        for s in range(SLOTS):
                            gather(p, s, turn)
                    continue
                pool.wait_ge(sums_zero, 16 * G)
                scatter(0, 0, 0)
                scatter(0, 0, 1)
                with pool.Fori(0, TURNS - 1) as turn:
                    for s in range(SLOTS):
                        scatter_after(s, turn)
                for s in range(SLOTS):
                    scatter_after(s, TURNS - 1, last=s == SLOTS - 1)
                pool.sem_inc(sums_scattered)

        @block.scalar
        def _(act):
            asked = [0]

            def func(out_, in_, f, scale=1.0):
                asked[0] += 1
                act.wait_ge(act_asked, asked[0])
                act.activation(out_, in_, f, scale=scale).then_inc(act_done, 1)

            def stage(n, ka, kb):
                with act.Fori(0, BATCHES) as b:
                    act.wait_ge(turned, b + (n * BATCHES + 1))
                    if kb:
                        act.copy(nbt[0:kb, :], psA[0:kb, 1024:1024 + NB * P])
                    act.copy(nat[0:ka, :], psA[0:ka, 0:NB * P]).then_inc(turned_out, 1)

            act_norm = lambda: func(stat[:, 1, :], stat[:, 1, :], ACT.Sqrt)
            act_norm()
            stage(0, RF, F)
            stage(1, RF, F)
            func(ta[:, 0:WINDOWS * F], tb[:, :], ACT.Exp)
            func(stat[:, 1, :], stat[:, 0, :], ACT.Ln)
            act_norm()
            stage(2, RF, F)
            stage(3, 2 * F, 0)
            stage(4, 2 * F, 0)
            act_norm()
            with act.Fori(0, TURNS) as turn:
                for s in range(SLOTS):
                    act.wait_ge(outer_turned, turn * SLOTS + s + 1)
                    act.copy(outerT, psA[:, :]).then_inc(outer_out, 1)
                    act.wait_ge(msg_product, turn * SLOTS + s + 1)
                    act.activation(msg[:, s % 2, :], psB[:, 0:G * F], ACT.Silu, scale=float(RF) ** -0.5).then_inc(msg_ready, 1)
            stage(5, F, 0)
            stage(6, RF, 0)
            stage(7, RF, 0)
            func(tb[:, :], tb[:, :], ACT.Silu, float(F * F) ** -0.5)
            stage(8, F, 0)
            act_norm()
            stage(9, RF, 0)
            stage(10, F, F)
            gates = flatS[:, 0:WINDOWS * 4 * F].rearrange("p (w k) -> p w k", k=4 * F)
            func(gates[:, :, 0:2 * F], gates[:, :, 0:2 * F], ACT.Sigmoid)
            func(gates[:, :, 2 * F:3 * F], gates[:, :, 2 * F:3 * F], ACT.Tanh)

        @block.tensor
        def _(pe):
            pe.wait_ge(constants_in, n_constants)
            pe.wait_ge(iotas, 8)
            pe.wait_ge(spans_ready, 1)

            def own_rows(p, s, turn):
                pe.wait_ge(fine_ready, turn * SLOTS + (hybrid(p) * GROUPS + s + 1))
                for t in range(OWN):
                    for way in range(WAYS):
                        for k in range(PARTS):
                            mm = pe.matmul(gathered_rows(s, t), fine[:, s % 2, way, t * P:(t + 1) * P], block_parts[:, :, way, k, :],
                                           start=t % 2 == 0 and way == 0 and k == 0, stop=True, skip_group_check=True)
                mm.then_inc(own_gathered, 1)

            def conv(p):
                width = SW if p == 0 else RF

                def sum_frame(s):
                    for t in range(G):
                        mm = pe.matmul(psC[:, 0:width], onehot[:, t, :], expanded[:, s % 2, t, 0:width],
                                       start=(t == 0), stop=(t == G - 1))
                    return mm

                def group(s, turn, last=False):
                    g = turn * SLOTS + s
                    pe.wait_ge(expanded_ready[s], turn + (p * TURNS + 2))
                    more = pe.value_load(spans[0:1, bass.ds(g, 1), 3], min_val=0, max_val=WINDOWS - 1)
                    extras = pe.value_load(spans[0:1, bass.ds(g, 1), 4], min_val=0, max_val=GROUPS * WINDOWS)
                    pe.wait_ge(first_ready[p], g + 1)
                    sum_frame(s).then_inc(first_done[p], 1)
                    with pe.If(more > 0):
                        with pe.Fori(1, more + 1) as i:
                            pe.wait_ge(more_ready[p], extras + i)
                            sum_frame(s).then_inc(more_done[p], 1)
                    if own(p) and not (last and s >= 2):
                        own_rows(p, (s + 2) % SLOTS, turn + (s + 2) // SLOTS)

                if own(p):
                    own_rows(p, 0, 0)
                    own_rows(p, 1, 0)
                with pe.Fori(0, TURNS - 1) as turn:
                    for s in range(SLOTS):
                        group(s, turn)
                for s in range(SLOTS):
                    group(s, TURNS - 1, last=True)

            def stage(n, ka, wa, kb=0, wb=None, cols=F):
                st = 128 if cols > 64 else 64
                with pe.Fori(0, BATCHES) as b:
                    pe.wait_ge(operands_ready, b + (n * BATCHES + 1))
                    for j in range(NB):
                        if kb:
                            pe.transpose(psA[0:kb, 1024 + j * P:1024 + (j + 1) * P], nb[:, j * kb:(j + 1) * kb], ident[:, :])
                        mm = pe.transpose(psA[0:ka, j * P:(j + 1) * P], na[:, j * ka:(j + 1) * ka], ident[:, :])
                    mm.then_inc(turned, 1)
                    pe.wait_ge(turned_out, b + (n * BATCHES + 1))
                    for j in range(NB):
                        mm = pe.matmul(psB[:, j * st:j * st + cols], nat[0:ka, j * P:(j + 1) * P], W(wa), start=True, stop=not kb)
                        if kb:
                            mm = pe.matmul(psB[:, j * st:j * st + cols], nbt[0:kb, j * P:(j + 1) * P], W(wb), start=False, stop=True)
                    mm.then_inc(product_done, 1)

            conv(0)
            stage(0, RF, "a1", F, "ar1")
            conv(1)
            stage(1, RF, "a2", F, "ar2")
            conv(2)
            stage(2, RF, "b1", F, "br1", cols=2 * F)
            stage(3, 2 * F, "br2")
            stage(4, 2 * F, "b2", cols=RF)
            conv(3)

            def target_rows(s, turn):
                g = turn * SLOTS + s
                lo = pe.value_load(spans[0:1, bass.ds(g, 1), 0], min_val=0, max_val=WINDOWS - 1)
                more = pe.value_load(spans[0:1, bass.ds(g, 1), 1], min_val=0, max_val=WINDOWS - 1)
                extras = pe.value_load(spans[0:1, bass.ds(g, 1), 2], min_val=0, max_val=GROUPS * WINDOWS)

                def pair(columns, win, first):
                    for t in range(G):
                        mm = pe.matmul(row_parts[:, t // HALF, t % HALF, :, :].rearrange("p k f -> p (k f)"),
                                       columns[:, t * P:(t + 1) * P],
                                       hparts[:, bass.ds(win, 1), :, :].rearrange("p w k f -> p (w k f)"),
                                       start=first and t % HALF == 0, stop=True, skip_group_check=True)
                    return mm

                pe.wait_ge(target_ready, g + 1)
                pair(target, lo, True).then_inc(target_used, 1)
                with pe.If(more > 0):
                    with pe.Fori(1, more + 1) as i:
                        pe.wait_ge(extra_ready, extras + i)
                        pair(extra_target, within(lo + i, WINDOWS - 1), False).then_inc(extra_used, 1)

            def turn_outer(s, turn):
                pe.wait_ge(expanded_ready[s], turn + (TP * TURNS + 2))
                for t in range(G):
                    mm = pe.transpose(psA[:, t * P:(t + 1) * P], outer[:, t * P:(t + 1) * P], ident[:, :])
                mm.then_inc(outer_turned, 1)

            def messages(s, turn, last=False):
                after = (s + 1) % SLOTS, turn + (s + 1) // SLOTS
                if not last:
                    target_rows(*after)
                pe.wait_ge(outer_out, turn * SLOTS + s + 1)
                for t in range(G):
                    mm = pe.matmul(psB[:, t * F:(t + 1) * F], outerT[:, t * P:(t + 1) * P], W("mtp"), start=True, stop=True)
                mm.then_inc(msg_product, 1)
                if not last:
                    turn_outer(*after)
                pe.wait_ge(parts_ready, turn * SLOTS + s + 1)
                pe.wait_ge(same_ready, turn * SLOTS + s + 1)
                for t in range(G):
                    for k in range(PARTS):
                        mm = pe.matmul(psC[:, t * F:(t + 1) * F], same[:, t, :], msg_parts[:, k, t * F:(t + 1) * F],
                                       start=t == 0 and k == 0, stop=True, skip_group_check=True)
                mm.then_inc(same_summed, 1)

            pe.sem_inc(extra_used)
            target_rows(0, 0)
            turn_outer(0, 0)
            with pe.Fori(0, TURNS - 1) as turn:
                for s in range(SLOTS):
                    messages(s, turn)
            for s in range(SLOTS):
                messages(s, TURNS - 1, last=s == SLOTS - 1)
            stage(5, F, "mlin")
            stage(6, RF, "utp0")
            stage(7, RF, "utp1")
            stage(8, F, "ulin")
            conv(5)
            stage(9, RF, "emb")
            stage(10, F, "gi", F, "gh", cols=4 * F)

        @block.vector
        def _(dve):
            steps, asked = [0], [0]

            def step(ins):
                steps[0] += 1
                ins.then_inc(dve_steps, 1)
                dve.wait_ge(dve_steps, steps[0])

            def ask(ins):
                asked[0] += 1
                ins.then_inc(act_asked, 1)
                dve.wait_ge(act_done, asked[0])

            def over(ap, n):
                return ap.unsqueeze(2).to_broadcast([P, ap.shape[1], n])

            def cols(t, k):
                return t[:, 0:WINDOWS * k].rearrange("p (w k) -> p w k", k=k)

            x3 = xs[:, :, :]
            h3, h32 = cols(hs, F), cols(hs, 2 * F)
            t3, t32 = cols(ta, F), cols(ta, 2 * F)
            u3 = cols(tb, F)
            S4 = S[:, 0:WINDOWS, 0:RF].rearrange("p w (r f) -> p w r f", r=R)

            def settle():
                step(dve.tensor_copy(none[:, :], spare[:, :]))

            def layernorm():
                step(dve.tensor_reduce(stat[:, 0, :], x3, AX.X, ALU.add))
                step(dve.tensor_scalar(stat[:, 0, :], stat[:, 0, :], 1.0 / F, None, ALU.mult))
                step(dve.tensor_tensor(t3, x3, over(stat[:, 0, :], F), ALU.subtract))
                step(dve.tensor_tensor(u3, t3, t3, ALU.mult))
                step(dve.tensor_reduce(stat[:, 1, :], u3, AX.X, ALU.add))
                ask(dve.tensor_scalar(stat[:, 1, :], stat[:, 1, :], 1.0 / F, EPS, ALU.mult, ALU.add))
                step(dve.reciprocal(stat[:, 0, :], stat[:, 1, :]))
                step(dve.tensor_tensor(t3, t3, over(stat[:, 0, :], F), ALU.mult))
                dve.tensor_scalar(h3, t3, 0.0, None, ALU.max).then_inc(h_ready, 1)

            def clear_sums():
                step(dve.memset(flatS, 0.0))

            def split_rows():
                settle()
                step(dve.tensor_copy(hparts[:, 0:WINDOWS, 0, :], h3))
                step(dve.tensor_tensor(t3, h3, hparts[:, 0:WINDOWS, 0, :], ALU.subtract))
                step(dve.tensor_copy(hparts[:, 0:WINDOWS, 1, :], t3))
                step(dve.tensor_tensor(hparts[:, 0:WINDOWS, 2, :], t3, hparts[:, 0:WINDOWS, 1, :], ALU.subtract))

            def expand(p, s, turn):
                dve.wait_ge(rows_in[CONV.index(p) // 3][s], turn * landed(p) + (landed(p) + landed_before(p)))
                dve.tensor_tensor(expanded[:, s % 2, :, RF:SW], over(rec[:, s, TYPE, :], R),
                                  iota_r[:, :].unsqueeze(1).to_broadcast([P, G, R]), ALU.is_equal).then_inc(masks_ready, 1)
                dve.wait_ge(masks_ready, turn * SLOTS + (CONV.index(p) * GROUPS + s + 1))
                dve.tensor_tensor(expanded[:, s % 2, :, 0:RF].rearrange("p t (r f) -> p t r f", r=R),
                                  rows[:, s, :, :].unsqueeze(2).to_broadcast([P, G, R, F]),
                                  expanded[:, s % 2, :, RF:SW].unsqueeze(3).to_broadcast([P, G, R, F]),
                                  ALU.mult).then_inc(expanded_ready[s], 1)

            def frame_columns(s, ready):
                dve.tensor_tensor(onehot[:, :, :], frame[:, :].unsqueeze(1).to_broadcast([P, G, P]),
                                  over(rec[:, s, DST, :], P), ALU.is_equal).then_inc(ready, 1)

            def first_frame(p, g, s):
                dve.tensor_scalar(wraps[:, :], iota_n[:, :], low_place[:, bass.ds(g, 1)], float(P), ALU.is_lt, ALU.mult
                                  ).then_inc(frame_steps[p], 1)
                dve.wait_ge(frame_steps[p], g * 2 + 1)
                dve.scalar_tensor_tensor(out=frame[:, :], in0=wraps[:, :], scalar=low_window[:, bass.ds(g, 1)],
                                         in1=iota_n[:, :], op0=ALU.add, op1=ALU.add).then_inc(frame_steps[p], 1)
                dve.wait_ge(frame_steps[p], g * 2 + 2)
                frame_columns(s, first_ready[p])

            def next_frame(p, s, k):
                dve.tensor_scalar(frame[:, :], frame[:, :], float(P), None, ALU.add).then_inc(more_frames[p], 1)
                dve.wait_ge(more_frames[p], k)
                frame_columns(s, more_ready[p])

            def add_frame(p, g, win, done, k):
                width = SW if p == 0 else RF
                dve.wait_ge(done[p], k)
                for window, mask in ((win, kept), (win + 1, wrapped)):
                    at = S[:, bass.ds(window, 1), 0:width].rearrange("p a b -> p (a b)")
                    dve.scalar_tensor_tensor(out=at, in0=psC[:, 0:width], scalar=mask[:, bass.ds(g, 1)], in1=at,
                                             op0=ALU.mult, op1=ALU.add)

            def places_of(p, s, turn):
                dve.wait_ge(place_in[s], turn * 16 + 16 * (hybrid(p) * TURNS + 1))
                for way in range(WAYS):
                    ins = dve.tensor_scalar(fine[:, s % 2, way, :], place[:, s, :], node_of[:, way:way + 1], None, ALU.is_equal)
                ins.then_inc(fine_ready, 1)

            def pick(p, s, turn):
                k = (turn * SLOTS + (hybrid(p) * GROUPS + s)) * 2
                dve.wait_ge(rec_in[s], turn * 16 + 16 * (p * TURNS + 1))
                dve.tensor_tensor(block_of[:, :, :], over(rec[:, s, BLOCK, G - OWN:G], BLOCKS),
                                  iota_n[:, 0:BLOCKS].unsqueeze(1).to_broadcast([P, OWN, BLOCKS]), ALU.is_equal).then_inc(pick_steps, 1)
                dve.wait_ge(pick_steps, k + 1)
                dve.wait_ge(own_gathered, turn * SLOTS + (hybrid(p) * GROUPS + s + 1))
                for t in range(0, OWN, 2):
                    n = min(2, OWN - t)
                    at = s % 2 * 1024 + t // 2 * 512
                    ins = dve.tensor_tensor(picked[:, t:t + n, :, :],
                                            psA[:, at:at + n * BLOCKS * F].rearrange("p (t b f) -> p t b f", t=n, f=F),
                                            block_of[:, t:t + n, :].unsqueeze(3).to_broadcast([P, n, BLOCKS, F]), ALU.mult)
                ins.then_inc(pick_steps, 1)
                dve.wait_ge(pick_steps, k + 2)
                dve.tensor_reduce(rows[:, s, G - OWN:G, :], picked[:, :, :, :].rearrange("p t b f -> p t f b"), AX.X, ALU.add)

            def conv(p):
                def group(s, turn, last=False):
                    g = turn * SLOTS + s
                    lo = dve.value_load(spans[0:1, bass.ds(g, 1), 0], min_val=0, max_val=WINDOWS - 1)
                    more = dve.value_load(spans[0:1, bass.ds(g, 1), 3], min_val=0, max_val=WINDOWS - 1)
                    extras = dve.value_load(spans[0:1, bass.ds(g, 1), 4], min_val=0, max_val=GROUPS * WINDOWS)
                    first_frame(p, g, s)
                    if own(p) and not (last and s >= 2):
                        places_of(p, (s + 2) % SLOTS, turn + (s + 2) // SLOTS)
                    if not (last and s == SLOTS - 1):
                        after = (s + 1) % SLOTS, turn + (s + 1) // SLOTS
                        if own(p):
                            pick(p, *after)
                        expand(p, *after)
                    add_frame(p, g, lo, first_done, g + 1)
                    with dve.If(more > 0):
                        with dve.Fori(1, more + 1) as i:
                            next_frame(p, s, extras + i)
                            add_frame(p, g, within(lo + i, WINDOWS - 1), more_done, extras + i)
                    dve.sem_inc(slot_free[s])

                if own(p):
                    split_rows()
                    places_of(p, 0, 0)
                    places_of(p, 1, 0)
                    pick(p, 0, 0)
                expand(p, 0, 0)
                with dve.Fori(0, TURNS - 1) as turn:
                    for s in range(SLOTS):
                        group(s, turn)
                for s in range(SLOTS):
                    group(s, TURNS - 1, last=True)

            def stage(n, load_a, load_b, store, width):
                st = 128 if width > 64 else 64
                with dve.Fori(0, BATCHES) as b:
                    w0 = b * NB
                    if load_b:
                        load_b(w0)
                    load_a(w0).then_inc(operands_ready, 1)
                    dve.wait_ge(product_done, b + (n * BATCHES + 1))
                    store(w0, psB[:, 0:NB * st].rearrange("p (w k) -> p w k", k=st)[:, :, 0:width])

            def batch(t, w0):
                return t[:, bass.ds(w0, NB), :]

            def from_sums(w0):
                return dve.tensor_tensor(na[:, :].rearrange("p (w r f) -> p w r f", w=NB, r=R), S4[:, bass.ds(w0, NB), :, :],
                                         batch(inv, w0).unsqueeze(3).to_broadcast([P, NB, R, F]), ALU.mult)

            def from_plain_sums(w0):
                return dve.tensor_copy(na[:, :].rearrange("p (w k) -> p w k", w=NB), S[:, bass.ds(w0, NB), 0:RF])

            def from_tile(t, k, to=na):
                return lambda w0: dve.tensor_copy(to[:, 0:NB * k].rearrange("p (w k) -> p w k", w=NB), batch(t, w0))

            def plus(t, k, bias):
                return lambda w0, psum: dve.tensor_tensor(batch(t, w0), psum, bias.unsqueeze(1).to_broadcast([P, NB, k]), ALU.add)

            def times(t, scale):
                return lambda w0, psum: dve.tensor_scalar(batch(t, w0), psum, scale, None, ALU.mult)

            dve.memset(xs[:, WINDOWS - 1, :], 0.0).then_inc(cleared, 1)
            dve.memset(wt[:, WP["gi"][0]:WP["gh"][0] + 4 * F], 0.0).then_inc(cleared, 1)
            dve.memset(span[:, 3, :], 1.0)

            dve.memset(hparts[:, WINDOWS:, :, :], 0.0)
            masked = hs[:, :].bitcast(I32)
            dve.wait_ge(flat_in, 16)
            step(dve.tensor_scalar(masked, ta[:, :].bitcast(I32), WAYS * P - 1, None, ALU.bitwise_and))
            dve.tensor_copy(tb[:, :].bitcast(I16), masked).then_inc(places_built, 1)

            dve.wait_ge(iotas, 8)
            for c in range(CHUNKS):
                dve.wait_ge(edges_in[c], 48)
                e = edge_chunk(c)
                r = record_chunk(c)
                if c >= 2:
                    dve.wait_ge(records_out[c - 2], 16)
                ev = e.rearrange("p k (g t) -> p k g t", t=G)
                dve.tensor_scalar(r[:, :, SRC_ROW, :], ev[:, 0], P - 1, None, ALU.bitwise_and)
                step(dve.tensor_scalar(r[:, :, TYPE_ROW, :], ev[:, 0], 7, None, ALU.logical_shift_right))
                step(dve.tensor_reduce(ext[:, 0, c * CG:(c + 1) * CG], ev[:, 1], AX.X, ALU.max))
                step(dve.tensor_reduce(ext[:, 1, c * CG:(c + 1) * CG], ev[:, 1], AX.X, ALU.min))
                step(dve.scalar_tensor_tensor(out=r[:, :, SRC_ROW, :], in0=r[:, :, SRC_ROW, :], scalar=float(WINDOWS),
                                              in1=r[:, :, TYPE_ROW, :], op0=ALU.mult, op1=ALU.add))
                dve.scalar_tensor_tensor(out=r[:, :, TYPE_ROW, :], in0=r[:, :, SRC_ROW, :], scalar=float(R),
                                         in1=ev[:, 2], op0=ALU.mult, op1=ALU.add)
                dve.tensor_scalar(r[:, :, BLOCK, :], ev[:, 0], 10, None, ALU.logical_shift_right)
                dve.tensor_copy(r[:, :, DST, :], ev[:, 1])
                dve.tensor_copy(r[:, :, TYPE, :], ev[:, 2])
                dve.tensor_copy(r[:, :, SRC, :], ev[:, 0]).then_inc(records_built, 1)
            step(dve.tensor_scalar(ext[:, 1, :], ext[:, 1, :], -1.0, None, ALU.mult))
            dve.tensor_copy(none[:, :], spare[:, :]).then_inc(ext_ready, 1)
            for c in range(CHUNKS):
                dve.wait_ge(records_out[c], 16)
            dve.wait_ge(places_out, 16)
            dve.memset(flatS, 0.0).then_inc(cleared, 1)

            dve.wait_ge(extr_ready, 1)
            step(dve.tensor_scalar(extr[:, 1, :], extr[:, 1, :], -1.0, None, ALU.mult))
            step(dve.tensor_copy(lowest[:, :], extr[:, 1, :]))
            step(dve.tensor_scalar(lowest[:, :], lowest[:, :], P - 1, None, ALU.bitwise_and))
            step(dve.tensor_copy(low_place[:, :], lowest[:, :]))
            dve.tensor_tensor(low_window[:, :], extr[:, 1, :], low_place[:, :], ALU.subtract)
            dve.tensor_scalar(wrapped[:, :], low_place[:, :], node_of[:, 0:1], None, ALU.is_gt)
            dve.tensor_scalar(kept[:, :], low_place[:, :], node_of[:, 0:1], None, ALU.is_le)

            dve.tensor_copy(span_of[:, 0, :], extr[0:1, 1, :])
            dve.tensor_copy(span_of[:, 1, :], extr[0:1, 0, :])
            step(dve.tensor_tensor(span_of[:, 2, :], extr[0:1, 0, :], extr[0:1, 1, :], ALU.subtract))
            step(dve.tensor_scalar(span_of[:, :, :], span_of[:, :, :], 7, None, ALU.logical_shift_right))
            dve.tensor_copy(span[:, 0, :], span_of[:, 0, :])
            step(dve.tensor_copy(span[:, 1, :], span_of[:, 1, :]))
            dve.tensor_copy(spans[:, :, 0], span[:, 0, :])
            step(dve.tensor_tensor(span[:, 1, :], span[:, 1, :], span[:, 0, :], ALU.subtract))
            for at in (1, 3):
                step(dve.tensor_tensor_scan(span[:, 2, :], span[:, 3, :], span[:, 1, :], 0.0, ALU.mult, ALU.add))
                step(dve.tensor_tensor(span[:, 2, :], span[:, 2, :], span[:, 1, :], ALU.subtract))
                dve.tensor_copy(spans[:, :, at], span[:, 1, :])
                step(dve.tensor_copy(spans[:, :, at + 1], span[:, 2, :]))
                if at == 1:
                    step(dve.tensor_copy(span[:, 1, :], span_of[:, 2, :]))
            dve.tensor_copy(none[:, :], spare[:, :]).then_inc(spans_ready, 1)
            dve.wait_ge(spans_ready, 1)

            dve.wait_ge(x_in, 32)
            layernorm()
            dve.wait_ge(sums_zero, 16 * G)

            conv(0)
            settle()
            step(dve.tensor_scalar(inv[:, :, :], S[:, 0:WINDOWS, RF:SW], 1.0, None, ALU.max))
            step(dve.reciprocal(inv[:, :, :], inv[:, :, :]))
            dve.wait_ge(constants_in, n_constants)
            stage(0, from_sums, from_tile(h3, F, nb), plus(t3, F, B("ab1")), F)
            settle()
            dve.tensor_scalar(h3, t3, 0.0, None, ALU.max).then_inc(h_ready, 1)
            clear_sums()
            conv(1)
            settle()
            stage(1, from_sums, from_tile(h3, F, nb), plus(t3, F, B("ab2")), F)
            settle()
            step(dve.tensor_reduce(stat[:, 0, :], t3, AX.X, ALU.max))
            step(dve.tensor_tensor(u3, t3, over(stat[:, 0, :], F), ALU.subtract))
            step(dve.tensor_tensor(x3, x3, u3, ALU.add))
            ask(dve.tensor_copy(none[:, :], spare[:, :]))
            ask(dve.tensor_reduce(stat[:, 0, :], t3, AX.X, ALU.add))
            step(dve.tensor_tensor(x3, x3, over(stat[:, 1, :], F), ALU.subtract))
            layernorm()

            clear_sums()
            conv(2)
            settle()
            stage(2, from_sums, from_tile(h3, F, nb), plus(t32, 2 * F, B("bb1")), 2 * F)
            settle()
            step(dve.tensor_scalar(h32, t32, 0.0, None, ALU.max))
            stage(3, from_tile(h32, 2 * F), None, plus(u3, F, B("bb2")), F)
            Y = flatS[:, 0:WINDOWS * RF].rearrange("p (w k) -> p w k", k=RF)
            stage(4, from_tile(h32, 2 * F), None, lambda w0, psum: dve.tensor_copy(batch(Y, w0), psum), RF)
            dve.tensor_copy(none[:, :], spare[:, :]).then_inc(h_ready, 1)
            step(dve.tensor_tensor(x3, x3, u3, ALU.add))
            dve.wait_ge(table_out, 16 * 4)
            clear_sums()
            conv(3)
            settle()
            step(dve.tensor_tensor(S4, S4, inv[:, :, :].unsqueeze(3).to_broadcast([P, WINDOWS, R, F]), ALU.mult))
            for r in range(R):
                step(dve.tensor_tensor(x3, x3, S4[:, :, r, :], ALU.add))
            layernorm()

            def targets(s, turn):
                g = turn * SLOTS + s
                lo = dve.value_load(spans[0:1, bass.ds(g, 1), 0], min_val=0, max_val=WINDOWS - 1)
                more = dve.value_load(spans[0:1, bass.ds(g, 1), 1], min_val=0, max_val=WINDOWS - 1)
                extras = dve.value_load(spans[0:1, bass.ds(g, 1), 2], min_val=0, max_val=GROUPS * WINDOWS)

                def pair(columns, win):
                    return dve.tensor_scalar(columns, wide[:, s % 2, 1, :], node_of[:, bass.ds(win, 1)], None, ALU.is_equal)

                dve.wait_ge(wide_in[s % 2], turn * 64 + (s // 2 + 1) * 32)
                pair(target, lo).then_inc(target_ready, 1)
                with dve.If(more > 0):
                    with dve.Fori(1, more + 1) as i:
                        dve.wait_ge(extra_used, extras + i)
                        pair(extra_target, within(lo + i, WINDOWS - 1)).then_inc(extra_ready, 1)
                return extras + more

            def spread(s, turn, extras, first=False):
                dve.wait_ge(target_used, turn * SLOTS + s + 1)
                dve.wait_ge(extra_used, extras + 1)
                dve.wait_ge(attrs_in[s], turn * 16 + 16)
                if not first:
                    dve.wait_ge(outer_turned, turn * SLOTS + s)
                for half in range(2):
                    dve.tensor_reduce(rows[:, s, half * HALF:(half + 1) * HALF, :],
                                      row_parts[:, half].rearrange("p t k f -> p t f k"), AX.X, ALU.add).then_inc(rows_summed, 1)
                dve.wait_ge(rows_summed, (turn * SLOTS + s) * 2 + 2)
                dve.tensor_tensor(outer.rearrange("p (t j f) -> p t j f", t=G, j=R),
                                  rows[:, s, :, :].unsqueeze(2).to_broadcast([P, G, R, F]),
                                  attrs[:, s, :, :].unsqueeze(3).to_broadcast([P, G, R, F]),
                                  ALU.mult).then_inc(expanded_ready[s], 1)

            def same_sources(s, turn, last=False):
                k = turn * SLOTS + s
                after = (s + 1) % SLOTS, turn + (s + 1) // SLOTS
                if not last:
                    extras = targets(*after)
                dve.wait_ge(wide_in[s % 2], turn * 64 + (s // 2 + 1) * 32)
                dve.wait_ge(rec_in[s], turn * 16 + 16 * (TP * TURNS + 1))
                dve.tensor_tensor(same, wide[:, s % 2, 0, :].rearrange("p (t e) -> p t e", t=G),
                                  over(rec[:, s, SRC, :], P), ALU.is_equal).then_inc(same_ready, 1)
                dve.wait_ge(same_ready, k + 1)
                dve.sem_inc(wide_free[s % 2])
                if not last:
                    spread(*after, extras)
                dve.tensor_tensor(earlier, same, before[:, :].unsqueeze(1).to_broadcast([P, G, P]),
                                  ALU.mult).then_inc(dup_steps, 1)
                dve.wait_ge(dup_steps, k * 4 + 1)
                dve.tensor_reduce(dup[:, 0, :], earlier, AX.X, ALU.add)
                dve.tensor_scalar(dup[:, 1, :], rec[:, s, SRC_ROW, :], spare[:, 0:1], -1.0, ALU.subtract,
                                  ALU.mult).then_inc(dup_steps, 1)
                dve.wait_ge(msg_ready, k + 1)
                dve.tensor_copy(msg_parts[:, 0, :], msg[:, s % 2, :]).then_inc(split_steps, 1)
                dve.wait_ge(dup_steps, k * 4 + 2)
                dve.scalar_tensor_tensor(out=dup[:, 2, :], in0=dup[:, 0, :], scalar=0.0, in1=dup[:, 1, :],
                                         op0=ALU.is_gt, op1=ALU.mult).then_inc(dup_steps, 1)
                dve.wait_ge(split_steps, k * 3 + 1)
                dve.tensor_tensor(msg_rest[:, :], msg[:, s % 2, :], msg_parts[:, 0, :], ALU.subtract).then_inc(split_steps, 1)
                dve.wait_ge(dup_steps, k * 4 + 3)
                dve.wait_ge(scatter_free[s], turn + 1)
                dve.tensor_tensor(scat[:, s, :], dup[:, 2, :], rec[:, s, SRC_ROW, :], ALU.add).then_inc(dup_steps, 1)
                dve.wait_ge(split_steps, k * 3 + 2)
                dve.tensor_copy(msg_parts[:, 1, :], msg_rest[:, :]).then_inc(split_steps, 1)
                dve.wait_ge(split_steps, k * 3 + 3)
                dve.tensor_tensor(msg_parts[:, 2, :], msg_rest[:, :], msg_parts[:, 1, :], ALU.subtract).then_inc(parts_ready, 1)
                dve.wait_ge(dup_steps, k * 4 + 4)
                dve.wait_ge(same_summed, k + 1)
                dve.tensor_copy(summed[:, s, :], psC[:, 0:G * F]).then_inc(summed_ready[s], 1)
                dve.sem_inc(slot_free[s])

            split_rows()
            spread(0, 0, targets(0, 0), first=True)
            with dve.Fori(0, TURNS - 1) as turn:
                for s in range(SLOTS):
                    same_sources(s, turn)
            for s in range(SLOTS):
                same_sources(s, TURNS - 1, last=s == SLOTS - 1)
            T8 = flatS[:, 0:(G // 2) * WINDOWS * F].rearrange("p (i k) -> p i k", i=G // 2)
            for half in range(2):
                dve.wait_ge(sums_in[half], 16 * (G // 2))
                for i in range(G // 2):
                    if half == 0 and i == 0:
                        step(dve.tensor_copy(tb[:, :], T8[:, 0, :]))
                    else:
                        step(dve.tensor_tensor(tb[:, :], tb[:, :], T8[:, i, :], ALU.add))
                if half == 0:
                    dve.sem_inc(sums_read)
            stage(5, from_tile(u3, F), None, times(t3, float(F) ** -0.5), F)
            settle()
            Z = flatS[:, 0:WINDOWS * RF].rearrange("p (w i f) -> p w i f", i=R, f=F)
            Z3 = flatS[:, 0:WINDOWS * RF].rearrange("p (w k) -> p w k", k=RF)
            v3 = cols(hs[:, WINDOWS * F:], F)
            for half in range(2):
                step(dve.tensor_tensor(Z, h3[:, :, half * R:(half + 1) * R].unsqueeze(3).to_broadcast([P, WINDOWS, R, F]),
                                       t3.unsqueeze(2).to_broadcast([P, WINDOWS, R, F]), ALU.mult))
                to = (u3, v3)[half]
                stage(6 + half, from_tile(Z3, RF), None, lambda w0, psum, to=to: dve.tensor_copy(batch(to, w0), psum), F)
                settle()
            ask(dve.tensor_tensor(u3, u3, v3, ALU.add))
            stage(8, from_tile(u3, F), None, times(t3, float(F) ** -0.5), F)
            settle()
            step(dve.tensor_tensor(t3, t3, h3, ALU.add))
            step(dve.tensor_tensor(x3, x3, t3, ALU.add))
            layernorm()

            clear_sums()
            dve.tensor_tensor(bg[:, 0:2 * F], B("ih", 0, 2 * F), B("hh", 0, 2 * F), ALU.add)
            dve.tensor_copy(bg[:, 2 * F:3 * F], B("ih", 2 * F))
            step(dve.tensor_copy(bg[:, 3 * F:4 * F], B("hh", 2 * F)))
            conv(5)
            settle()
            stage(9, from_plain_sums, None, times(t3, 1.0), F)
            settle()
            gates = flatS[:, 0:WINDOWS * 4 * F].rearrange("p (w k) -> p w k", k=4 * F)
            stage(10, from_tile(t3, F), from_tile(h3, F, nb), plus(gates, 4 * F, bg[:, :]), 4 * F)
            ask(dve.tensor_copy(none[:, :], spare[:, :]))
            step(dve.tensor_tensor(t3, gates[:, :, 0:F], gates[:, :, 3 * F:4 * F], ALU.mult))
            ask(dve.tensor_tensor(gates[:, :, 2 * F:3 * F], gates[:, :, 2 * F:3 * F], t3, ALU.add))
            new = gates[:, :, 2 * F:3 * F]
            step(dve.tensor_tensor(t3, h3, new, ALU.subtract))
            step(dve.tensor_tensor(t3, t3, gates[:, :, F:2 * F], ALU.mult))
            step(dve.tensor_tensor(t3, t3, new, ALU.add))
            dve.tensor_tensor(x3, x3, t3, ALU.add).then_inc(out_ready, 1)


def kernel(**inputs):
    import numpy as np
    import concourse.bacc as bacc
    from concourse.bass_utils import run_bass_kernel_spmd

    def edges(name, fill):
        a = np.asarray(inputs[name])
        return np.concatenate([a, np.full((EPAD - EDGES,) + a.shape[1:], fill, a.dtype)])

    def tiles(a):
        return np.ascontiguousarray(a.reshape(EC, P, -1).transpose(1, 0, 2).reshape(P, -1))

    def get(name, shape=None, perm=None):
        a = np.asarray(inputs[name])
        a = a if perm is None else a.transpose(perm)
        return np.ascontiguousarray(a if shape is None else a.reshape(shape))

    none = NPAD - 1
    src, dst = edges("src", none), edges("dst", none)
    arrays = {
        "x": get("x"), "src": tiles(src), "dst": tiles(dst), "typ": tiles(edges("edge_type_8", 0)),
        "src_flat": src, "dst_flat": dst, "attr": tiles(edges("edge_attr_8", 0)),
        "a1": get("L0_gnn_W1", (RF, F)), "ar1": get("L0_gnn_root1"), "a2": get("L0_gnn_W2", (RF, F)), "ar2": get("L0_gnn_root2"),
        "b1": get("L1_gnn_W1", (RF, 2 * F)), "br1": get("L1_gnn_root1"),
        "b2": get("L1_gnn_W2", (2 * F, RF), (1, 0, 2)), "br2": get("L1_gnn_root2"),
        "mtp": get("L2_gnn_W_msg_tp", (RF, F), (1, 0, 2)), "mlin": get("L2_gnn_W_msg_lin"),
        "utp0": get("L2_gnn_W_upd_tp", (F * F, F))[0:RF], "utp1": get("L2_gnn_W_upd_tp", (F * F, F))[RF:],
        "ulin": get("L2_gnn_W_upd_lin"),
        "emb": np.ascontiguousarray(get("L3_gnn_edge_emb", (R, F, F)).transpose(0, 2, 1).reshape(RF, F)),
        "gi": get("L3_gnn_w_ih", None, (1, 0)), "gh": get("L3_gnn_w_hh", None, (1, 0)),
        "ab1": get("L0_gnn_b1"), "ab2": get("L0_gnn_b2"), "bb1": get("L1_gnn_b1"), "bb2": get("L1_gnn_b2"),
        "ih": get("L3_gnn_b_ih"), "hh": get("L3_gnn_b_hh"),
    }
    nc = bacc.Bacc("TRN2", target_bir_lowering=False, num_devices=1)
    d = {n: nc.dram_tensor(f"in_{n}", a.shape, mybir.dt.from_np(a.dtype), kind="ExternalInput").ap() for n, a in arrays.items()}
    out = nc.dram_tensor("out_x", (NODES, F), F32, kind="ExternalOutput").ap()
    gnn_kernel(nc, *(d[n] for n in ("x", "src", "dst", "typ", "src_flat", "dst_flat", "attr")),
               {n: d[n] for n, *_ in WEIGHTS}, {n: d[n] for n, _ in BIASES}, out)
    r = run_bass_kernel_spmd(nc, [{f"in_{n}": a for n, a in arrays.items()}], core_ids=[0])
    return r.results[0]["out_x"]
```

```python
from contextlib import ExitStack

import concourse.bass as bass
from concourse import mybir

F32 = mybir.dt.float32
BF16 = mybir.dt.bfloat16
I32 = mybir.dt.int32
I16 = mybir.dt.int16
ALU = mybir.AluOpType
ACT = mybir.ActivationFunctionType
AX = mybir.AxisListType

P = 128
NODES = 12500
EDGES = 400000
F = 16
R = 8
WINDOWS = -(-NODES // P)
NPAD = WINDOWS * P
TAIL = NODES - (WINDOWS - 1) * P
G = 16
GE = G * P
SLOTS = 4
TURNS = -(-EDGES // (GE * SLOTS))
GROUPS = TURNS * SLOTS
EPAD = GROUPS * GE
EC = EPAD // P
FIELDS = 6
SRC_ROW, TYPE_ROW, DST, TYPE, SRC, BLOCK = range(FIELDS)
REC = FIELDS * G
CHUNKS = 4
CG = GROUPS // CHUNKS
RF = R * F
SW = RF + R
NB = 7
BATCHES = WINDOWS // NB
OWN = 4
WAYS = 8
BLOCKS = -(-WINDOWS // WAYS)
HALF = G // 2
PARTS = 3
EPS = 1e-5
PASSES = 6
CONV = [0, 1, 2, 3, 5]
TP = 4
BY_TYPE = 3


def own(p):
    return 0 if p == BY_TYPE else OWN


def landed(p):
    return 16 * (G - own(p))


def landed_before(p):
    i = CONV.index(p)
    return sum(landed(q) for q in CONV[i - i % 3:i]) * TURNS


WEIGHTS = [("a1", 128, 16), ("a2", 128, 16), ("b1", 128, 32), ("b2", 32, 128), ("br2", 32, 16), ("mtp", 128, 16),
           ("utp0", 128, 16), ("utp1", 128, 16), ("emb", 128, 16)]
DIAGONAL = [("ar1", 16), ("ar2", 16), ("br1", 32), ("mlin", 16), ("ulin", 16), ("gi", 64), ("gh", 64)]
BIASES = [("ab1", 16), ("ab2", 16), ("bb1", 32), ("bb2", 16), ("ih", 48), ("hh", 48)]


def places(list_of_sizes):
    at, found = 0, {}
    for name, *_, n in list_of_sizes:
        found[name] = (at, n)
        at += n
    return found, at


def gnn_kernel(nc, x, src, dst, typ, src_flat, dst_flat, attr, w, biases, out):
    WP, WCOLS = places(WEIGHTS)
    DP, DCOLS = places([(name, NB * n) for name, n in DIAGONAL])
    BP, BCOLS = places(BIASES)
    with ExitStack() as ctx:
        def sb(name, shape, dt=F32):
            return ctx.enter_context(nc.sbuf_tensor(name, shape, dt))

        def ps(name, shape):
            return ctx.enter_context(nc.psum_tensor(name, shape, F32))

        def sem(name):
            return ctx.enter_context(nc.semaphore(name))

        def sems(name, n):
            return [sem(f"{name}{i}") for i in range(n)]

        table = {p: nc.dram_tensor(f"table{p}", (NPAD, F), F32, kind="Internal").ap() for p in CONV if p != 3}
        table[3] = nc.dram_tensor("table3", (NPAD * R, F), F32, kind="Internal").ap()
        place_flat = nc.dram_tensor("place_flat", (EPAD,), I16, kind="Internal").ap()
        records = nc.dram_tensor("records", (P, GROUPS * REC), I32, kind="Internal").ap()
        sums = [nc.dram_tensor(f"sums{i}", (NPAD + P, F), F32, kind="Internal").ap() for i in range(G)]

        xs = sb("xs", [P, WINDOWS, F])
        hs = sb("hs", [P, WINDOWS * 2 * F])
        S = sb("S", [P, WINDOWS + 1, SW])
        ta = sb("ta", [P, WINDOWS * 2 * F])
        tb = sb("tb", [P, WINDOWS * F])
        inv = sb("inv", [P, WINDOWS, R])
        stat = sb("stat", [P, 2, WINDOWS])
        rec = sb("rec", [P, SLOTS, FIELDS, G], I32)
        rows = sb("rows", [P, SLOTS, G, F])
        expanded = sb("expanded", [P, 2, G, SW])
        onehot = sb("onehot", [P, G, P])
        frame = sb("frame", [P, P])
        wraps = sb("wraps", [P, P])
        none = sb("none", [P, 1])
        iota_n = sb("iota_n", [P, P])
        iota_r = sb("iota_r", [P, R])
        ident = sb("ident", [P, P])
        before = sb("before", [P, P], BF16)
        hparts = sb("hparts", [P, BLOCKS * WAYS, PARTS, F], BF16)
        msg_parts = sb("msg_parts", [P, PARTS, G * F], BF16)
        msg_rest = sb("msg_rest", [P, G * F])
        place = sb("place", [P, SLOTS, OWN * P], I16)
        fine = sb("fine", [P, 2, WAYS, OWN * P], BF16)
        block_of = sb("block_of", [P, OWN, BLOCKS])
        picked = sb("picked", [P, OWN, BLOCKS, F])
        spare = sb("spare", [P, 1])
        node_of = sb("node_of", [P, WINDOWS])
        wt = sb("wt", [P, WCOLS])
        diagonal = sb("diagonal", [NB * F, DCOLS])
        bt = sb("bt", [P, BCOLS])
        bg = sb("bg", [P, 4 * F])
        nb = sb("nb", [P, 2, 2, NB * F])
        nbt = sb("nbt", [NB * F, 2, 2, P])
        ext = sb("ext", [P, 2, GROUPS])
        extr = sb("extr", [P, 2, GROUPS])
        lowest = sb("lowest", [P, GROUPS], I32)
        low_place = sb("low_place", [P, GROUPS])
        low_window = sb("low_window", [P, GROUPS])
        kept = sb("kept", [P, GROUPS])
        wrapped = sb("wrapped", [P, GROUPS])
        span = sb("span", [1, 4, GROUPS])
        span_of = sb("span_of", [1, 3, GROUPS], I32)
        spans = sb("spans", [1, GROUPS, 5], I32)
        attrs = sb("attrs", [P, SLOTS, G, R])
        msg = sb("msg", [P, 2, G * F])
        summed = sb("summed", [P, SLOTS, G * F])
        scat = sb("scat", [P, SLOTS, G], I32)
        dup = sb("dup", [P, 3, G])

        psA = ps("psA", [P, 2048])
        psB = ps("psB", [P, 1536])
        psC = ps("psC", [P, 512])

        flatS = S[:, :, :].rearrange("p w f -> p (w f)")
        wide = flatS[:, 0:4 * GE].bitcast(I32).rearrange("p (b k e) -> p b k e", b=2, k=2)
        outerT = flatS[:, 4 * GE:5 * GE]
        earlier = flatS[:, 5 * GE:5 * GE + GE // 2].bitcast(BF16).rearrange("p (t e) -> p t e", t=G)
        outer = expanded[:, 0, :, :].rearrange("p t k -> p (t k)")[:, 0:GE]
        target = expanded[:, 1, :, :].rearrange("p t k -> p (t k)")[:, 0:GE // 2].bitcast(BF16)
        extra_target = ta[:, 0:GE // 2].bitcast(BF16)
        same = onehot[:, :, :].rearrange("p t e -> p (t e)")[:, 0:GE // 2].bitcast(BF16).rearrange("p (t e) -> p t e", t=G)
        fine_flat = fine[:, :, :, :].rearrange("p a w e -> p (a w e)").bitcast(F32)
        na = [fine_flat[:, i * NB * P:(i + 1) * NB * P] for i in range(2)]
        nat = [fine_flat[:, (2 + i) * NB * P:(3 + i) * NB * P] for i in range(2)]
        block_parts = hparts[:, :, :, :].rearrange("p (b w) k f -> p b w k f", w=WAYS)

        def gathered_rows(s, t):
            at = s % 2 * 1024 + t // 2 * 512 + t % 2 * BLOCKS * F
            return psA[:, at:at + BLOCKS * F]

        row_parts = psB[:, 512:1536].rearrange("p (b n) -> p b n", b=2)[:, :, 0:HALF * PARTS * F].rearrange(
            "p b (t k f) -> p b t k f", t=HALF, k=PARTS)

        def W(name):
            rows_of = {n: k for n, k, _ in WEIGHTS}
            at, n = WP[name]
            return wt[0:rows_of[name], at:at + n]

        def D(name):
            at, n = DP[name]
            return diagonal[:, at:at + n]

        def B(name, lo=0, hi=None):
            at, n = BP[name]
            return bt[:, at + lo:at + (n if hi is None else hi)]

        constants_in = sem("constants_in")
        x_in = sem("x_in")
        iotas = sem("iotas")
        edges_in = sems("edges_in", CHUNKS)
        records_built = sem("records_built")
        records_out = sems("records_out", CHUNKS)
        ext_ready = sem("ext_ready")
        extr_ready = sem("extr_ready")
        spans_ready = sem("spans_ready")
        cleared = sem("cleared")
        sums_zero = sem("sums_zero")
        dve_steps = sem("dve_steps")
        act_asked = sem("act_asked")
        act_done = sem("act_done")
        h_ready = sem("h_ready")
        table_out = sem("table_out")
        slot_free = sems("slot_free", SLOTS)
        rec_in = sems("rec_in", SLOTS)
        rows_in = [sems(f"rows_in_{k}_", SLOTS) for k in range(2)]
        masks_ready = sem("masks_ready")
        groups_begun = sem("groups_begun")
        expanded_ready = sems("expanded_ready", SLOTS)
        first_ready = {p: sem(f"first_ready{p}") for p in CONV}
        first_done = {p: sem(f"first_done{p}") for p in CONV}
        frame_steps = {p: sem(f"frame_steps{p}") for p in CONV}
        more_frames = {p: sem(f"more_frames{p}") for p in CONV}
        more_ready = {p: sem(f"more_ready{p}") for p in CONV}
        more_done = {p: sem(f"more_done{p}") for p in CONV}
        flat_in = sem("flat_in")
        places_built = sem("places_built")
        places_out = sem("places_out")
        place_in = sems("place_in", SLOTS)
        fine_ready = sem("fine_ready")
        own_gathered = sem("own_gathered")
        pick_steps = sem("pick_steps")
        operands_ready = sem("operands_ready")
        turned = sem("turned")
        turned_out = sem("turned_out")
        product_done = sem("product_done")
        batch_done = sem("batch_done")
        attrs_in = sems("attrs_in", SLOTS)
        wide_in = sems("wide_in", 2)
        wide_free = sems("wide_free", 2)
        target_ready = sem("target_ready")
        extra_ready = sem("extra_ready")
        target_used = sem("target_used")
        extra_used = sem("extra_used")
        outer_turned = sem("outer_turned")
        outer_out = sem("outer_out")
        msg_product = sem("msg_product")
        msg_ready = sem("msg_ready")
        parts_ready = sem("parts_ready")
        split_steps = sem("split_steps")
        rows_summed = sem("rows_summed")
        same_ready = sem("same_ready")
        same_summed = sem("same_summed")
        summed_ready = sems("summed_ready", SLOTS)
        scattered = [sems(f"scattered{half}_", SLOTS) for half in range(2)]
        scatter_free = sems("scatter_free", SLOTS)
        dup_steps = sem("dup_steps")
        sums_scattered = sem("sums_scattered")
        sums_in = sems("sums_in", 2)
        sums_read = sem("sums_read")
        out_ready = sem("out_ready")
        out_done = sem("out_done")

        n_constants = 16 * (len(WEIGHTS) + NB * (len(DIAGONAL) + 2) + len(BIASES))

        def hybrid(p):
            return len([q for q in CONV[:CONV.index(p)] if own(q)])

        def within(v, hi):
            return nc.s_assert_within(v, 0, hi, skip_runtime_bounds_check_because="the tables of spans hold windows alone")

        block = ctx.enter_context(nc.Block())

        def edge_chunk(c):
            return flatS[:, 0:3 * CG * G].bitcast(I32).rearrange("p (k e) -> p k e", k=3)

        def record_chunk(c):
            at = 3 * CG * G + (c % 2) * CG * REC
            return flatS[:, at:at + CG * REC].bitcast(I32).rearrange("p (g k t) -> p g k t", g=CG, k=FIELDS)

        def store_records(sp, c):
            sp.wait_ge(records_built, c + 1)
            sp.dma_start(records[:, c * CG * REC:(c + 1) * CG * REC],
                         record_chunk(c).rearrange("p g k t -> p (g k t)")).then_inc(records_out[c], 16)

        @block.sync
        def _(sp):
            sp.dma_start(xs[:, 0:WINDOWS - 1, :], x[0:(WINDOWS - 1) * P, :].rearrange("(w p) f -> p w f", p=P)).then_inc(x_in, 16)
            sp.wait_ge(cleared, 2)
            sp.dma_start(xs[0:TAIL, WINDOWS - 1, :], x[(WINDOWS - 1) * P:NODES, :]).then_inc(x_in, 16)
            sp.dma_start(ta[:, :].bitcast(I32), src_flat.rearrange("(p e) -> p e", p=P)).then_inc(flat_in, 16)
            for c in range(CHUNKS):
                if c:
                    store_records(sp, c - 1)
                for i, a in enumerate((src, dst, typ)):
                    sp.dma_start(edge_chunk(c)[:, i, :], a[:, c * CG * G:(c + 1) * CG * G]).then_inc(edges_in[c], 16)
            store_records(sp, CHUNKS - 1)
            sp.wait_ge(places_built, 1)
            sp.dma_start(place_flat.rearrange("(p e) -> p e", p=P), tb[:, :].bitcast(I16)).then_inc(places_out, 16)
            sp.wait_ge(cleared, 3)
            for i in range(G):
                sp.dma_start(sums[i].rearrange("(p t) f -> p (t f)", p=P), flatS[:, 0:(WINDOWS + 1) * F]).then_inc(sums_zero, 16)
            for s in range(SLOTS):
                sp.sem_inc(slot_free[s])
            for b in range(2):
                sp.sem_inc(wide_free[b])
            for c in range(CHUNKS):
                sp.wait_ge(records_out[c], 16)
            sp.wait_ge(places_out, 16)
            for p in range(PASSES):
                sp.wait_ge(h_ready, p + 1)
                if p == 3:
                    sp.dma_start(table[p].rearrange("(p t) f -> p (t f)", p=P), flatS[:, 0:WINDOWS * RF]).then_inc(table_out, 16)
                elif p != TP:
                    sp.dma_start(table[p].rearrange("(p t) f -> p (t f)", p=P), hs[:, 0:WINDOWS * F]).then_inc(table_out, 16)
                with sp.Fori(0, TURNS) as turn:
                    for s in range(SLOTS):
                        g = turn * SLOTS + s
                        sp.wait_ge(slot_free[s], turn + (p * TURNS + 1))
                        sp.dma_start(rec[:, s, :, :].rearrange("p k t -> p (k t)"),
                                     records[:, bass.ds(g * REC, REC)]).then_inc(rec_in[s], 16)
                        if p in CONV and own(p):
                            sp.dma_start(place[:, s, :], place_flat[bass.ds(g * GE + (G - OWN) * P, OWN * P)].partition_broadcast(P)
                                         ).then_inc(place_in[s], 16)
                        if p == TP:
                            sp.dma_start(attrs[:, s, :, :].rearrange("p t j -> p (t j)"),
                                         attr[:, bass.ds(g * (G * R), G * R)]).then_inc(attrs_in[s], 16)
                            sp.wait_ge(wide_free[s % 2], turn * 2 + (s // 2 + 1))
                            for k, flat in enumerate((src_flat, dst_flat)):
                                sp.dma_start(wide[:, s % 2, k, :],
                                             flat[bass.ds(g * GE, GE)].partition_broadcast(P)).then_inc(wide_in[s % 2], 16)
                if p == TP:
                    for half in range(2):
                        if half == 0:
                            sp.wait_ge(sums_scattered, 1)
                        else:
                            sp.wait_ge(sums_read, 1)
                        for i in range(G // 2):
                            sp.dma_start(flatS[:, i * WINDOWS * F:(i + 1) * WINDOWS * F],
                                         sums[half * (G // 2) + i][0:NPAD, :].rearrange("(p t) f -> p (t f)", p=P)
                                         ).then_inc(sums_in[half], 16)
            sp.wait_ge(out_ready, 1)
            sp.dma_start(out[0:(WINDOWS - 1) * P, :].rearrange("(w p) f -> p w f", p=P), xs[:, 0:WINDOWS - 1, :]).then_inc(out_done, 16)
            sp.dma_start(out[(WINDOWS - 1) * P:NODES, :], xs[0:TAIL, WINDOWS - 1, :]).then_inc(out_done, 16)
            sp.wait_ge(out_done, 32)

        @block.gpsimd
        def _(pool):
            pool.iota(iota_n[:, :], [[1, P]], base=0, channel_multiplier=0, allow_small_or_imprecise_dtypes=True).then_inc(iotas, 1)
            pool.iota(iota_r[:, :], [[1, R]], base=0, channel_multiplier=0, allow_small_or_imprecise_dtypes=True).then_inc(iotas, 1)
            pool.iota(node_of[:, :], [[P, WINDOWS]], base=0, channel_multiplier=1, allow_small_or_imprecise_dtypes=True).then_inc(iotas, 1)
            pool.iota(spare[:, :], [[1, 1]], base=NPAD, channel_multiplier=1, allow_small_or_imprecise_dtypes=True).then_inc(iotas, 1)
            pool.memset(ident[:, :], 0.0).then_inc(iotas, 1)
            pool.memset(before[:, :], 1.0).then_inc(iotas, 1)
            pool.wait_ge(iotas, 6)
            pool.affine_select(out=ident[:, :], in_=ident[:, :], compare_op=ALU.not_equal, fill=1.0, base=0,
                               pattern=[[-1, P]], channel_multiplier=1).then_inc(iotas, 1)
            pool.affine_select(out=before[:, :], in_=before[:, :], compare_op=ALU.is_gt, fill=0.0, base=0,
                               pattern=[[-1, P]], channel_multiplier=1).then_inc(iotas, 1)
            pool.wait_ge(ext_ready, 1)
            pool.partition_all_reduce(extr[:, :, :].rearrange("p a g -> p (a g)"), ext[:, :, :].rearrange("p a g -> p (a g)"),
                                      P, bass.bass_isa.ReduceOp.max).then_inc(extr_ready, 1)

            def gather(p, s, turn):
                pool.wait_ge(rec_in[s], turn * 16 + 16 * (p * TURNS + 1))
                pool.wait_ge(expanded_ready[s], turn + (p * TURNS + 1))
                pool.sem_inc(groups_begun)
                field = TYPE_ROW if p == BY_TYPE else SRC_ROW
                for t in range(G - own(p)):
                    pool.indirect_dma_start(out=rows[:, s, t, :], out_offset=None, in_=table[p],
                                            in_offset=bass.IndirectOffsetOnAxis(ap=rec[:, s, field, t:t + 1], axis=0)
                                            ).then_inc(rows_in[CONV.index(p) // 3][s], 16)

            def scatter(s, turn, half):
                pool.wait_ge(summed_ready[s], turn + 1)
                pool.sem_inc(groups_begun)
                for t in range(half * HALF, (half + 1) * HALF):
                    pool.indirect_dma_start(out=sums[t], out_offset=bass.IndirectOffsetOnAxis(ap=scat[:, s, t:t + 1], axis=0),
                                            in_=summed[:, s, t * F:(t + 1) * F], in_offset=None,
                                            compute_op=ALU.add).then_inc(scattered[half][s], 16)

            def scatter_after(s, turn, last=False):
                for half in range(2):
                    pool.wait_ge(scattered[half][s], turn * (16 * HALF) + 16 * HALF)
                    if half:
                        pool.sem_inc(scatter_free[s])
                    if not last:
                        scatter((s + 1) % SLOTS, turn + (s + 1) // SLOTS, half)

            for s in range(SLOTS):
                pool.sem_inc(expanded_ready[s])
                pool.sem_inc(scatter_free[s])
            for p in range(PASSES):
                if p != TP:
                    pool.wait_ge(table_out, 16 * (CONV.index(p) + 1))
                    with pool.Fori(0, TURNS) as turn:
                        for s in range(SLOTS):
                            gather(p, s, turn)
                    continue
                pool.wait_ge(sums_zero, 16 * G)
                scatter(0, 0, 0)
                scatter(0, 0, 1)
                with pool.Fori(0, TURNS - 1) as turn:
                    for s in range(SLOTS):
                        scatter_after(s, turn)
                for s in range(SLOTS):
                    scatter_after(s, TURNS - 1, last=s == SLOTS - 1)
                pool.sem_inc(sums_scattered)

        @block.scalar
        def _(act):
            for name, k, n in WEIGHTS:
                act.dma_start(W(name), w[name]).then_inc(constants_in, 16)
            for name, n in BIASES:
                act.dma_start(B(name), biases[name].partition_broadcast(P)).then_inc(constants_in, 16)
            act.wait_ge(cleared, 2)
            for name, n in DIAGONAL:
                for j in range(NB):
                    at = DP[name][0] + j * n
                    to = diagonal[j * F:(j + 1) * F, :]
                    if name in ("gi", "gh"):
                        act.dma_start(to[:, at:at + 2 * F], w[name][:, 0:2 * F]).then_inc(constants_in, 16)
                        new = at + 2 * F if name == "gi" else at + 3 * F
                        act.dma_start(to[:, new:new + F], w[name][:, 2 * F:3 * F]).then_inc(constants_in, 16)
                    else:
                        act.dma_start(to[:, at:at + n], w[name]).then_inc(constants_in, 16)
            asked = [0]

            def func(out_, in_, f, scale=1.0):
                asked[0] += 1
                act.wait_ge(act_asked, asked[0])
                act.activation(out_, in_, f, scale=scale).then_inc(act_done, 1)

            def stage(n, ka, narrow=0):
                with act.Fori(0, BATCHES // 2) as turn:
                    for half in range(2):
                        act.wait_ge(turned, turn * 2 + (n * BATCHES + half + 1))
                        for i in range(narrow):
                            copied = act.copy(nbt[:, half, i, :], psA[0:NB * F, 1024 + i * 512:1024 + i * 512 + P])
                        if ka:
                            copied = act.copy(nat[half][0:ka, :], psA[0:ka, 0:NB * P])
                        copied.then_inc(turned_out, 1)

            act_norm = lambda: func(stat[:, 1, :], stat[:, 1, :], ACT.Sqrt)
            act_norm()
            stage(0, RF, 1)
            stage(1, RF, 1)
            func(ta[:, 0:WINDOWS * F], tb[:, :], ACT.Exp)
            func(stat[:, 1, :], stat[:, 0, :], ACT.Ln)
            act_norm()
            stage(2, RF, 1)
            stage(3, 2 * F)
            stage(4, 2 * F)
            act_norm()
            with act.Fori(0, TURNS) as turn:
                for s in range(SLOTS):
                    act.wait_ge(outer_turned, turn * SLOTS + s + 1)
                    act.copy(outerT, psA[:, :]).then_inc(outer_out, 1)
                    act.wait_ge(msg_product, turn * SLOTS + s + 1)
                    act.activation(msg[:, s % 2, :], psB[:, 0:G * F], ACT.Silu, scale=float(RF) ** -0.5).then_inc(msg_ready, 1)
            stage(5, 0, 1)
            stage(6, RF)
            stage(7, RF)
            func(tb[:, :], tb[:, :], ACT.Silu, float(F * F) ** -0.5)
            stage(8, 0, 1)
            act_norm()
            stage(9, RF)
            stage(10, 0, 2)
            gates = flatS[:, 0:WINDOWS * 4 * F].rearrange("p (w k) -> p w k", k=4 * F)
            func(gates[:, :, 0:2 * F], gates[:, :, 0:2 * F], ACT.Sigmoid)
            func(gates[:, :, 2 * F:3 * F], gates[:, :, 2 * F:3 * F], ACT.Tanh)

        @block.tensor
        def _(pe):
            pe.wait_ge(iotas, 8)
            pe.wait_ge(spans_ready, 1)

            def own_rows(p, s, turn):
                pe.wait_ge(fine_ready, turn * SLOTS + (hybrid(p) * GROUPS + s + 1))
                for t in range(OWN):
                    for way in range(WAYS):
                        for k in range(PARTS):
                            mm = pe.matmul(gathered_rows(s, t), fine[:, s % 2, way, t * P:(t + 1) * P], block_parts[:, :, way, k, :],
                                           start=t % 2 == 0 and way == 0 and k == 0, stop=True, skip_group_check=True)
                mm.then_inc(own_gathered, 1)

            def conv(p):
                width = SW if p == 0 else RF

                def sum_frame(s):
                    for t in range(G):
                        mm = pe.matmul(psC[:, 0:width], onehot[:, t, :], expanded[:, s % 2, t, 0:width],
                                       start=(t == 0), stop=(t == G - 1))
                    return mm

                def group(s, turn, last=False):
                    g = turn * SLOTS + s
                    pe.wait_ge(expanded_ready[s], turn + (p * TURNS + 2))
                    more = pe.value_load(spans[0:1, bass.ds(g, 1), 3], min_val=0, max_val=WINDOWS - 1)
                    extras = pe.value_load(spans[0:1, bass.ds(g, 1), 4], min_val=0, max_val=GROUPS * WINDOWS)
                    pe.wait_ge(first_ready[p], g + 1)
                    sum_frame(s).then_inc(first_done[p], 1)
                    with pe.If(more > 0):
                        with pe.Fori(1, more + 1) as i:
                            pe.wait_ge(more_ready[p], extras + i)
                            sum_frame(s).then_inc(more_done[p], 1)
                    if own(p) and not (last and s >= 2):
                        own_rows(p, (s + 2) % SLOTS, turn + (s + 2) // SLOTS)

                if own(p):
                    own_rows(p, 0, 0)
                    own_rows(p, 1, 0)
                with pe.Fori(0, TURNS - 1) as turn:
                    for s in range(SLOTS):
                        group(s, turn)
                for s in range(SLOTS):
                    group(s, TURNS - 1, last=True)

            def stage(n, ka=0, wide=None, narrow=(), cols=F):
                def turn_batch(k, half):
                    pe.wait_ge(operands_ready, k + (n * BATCHES + 1))
                    for i in range(len(narrow)):
                        mm = pe.transpose(psA[0:NB * F, 1024 + i * 512:1024 + i * 512 + P], nb[:, half, i, :], ident[:, :])
                    for j in range(NB if wide else 0):
                        mm = pe.transpose(psA[0:ka, j * P:(j + 1) * P], na[half][:, j * ka:(j + 1) * ka], ident[:, :])
                    mm.then_inc(turned, 1)

                def product(k, half):
                    pe.wait_ge(batch_done, k + n * BATCHES)
                    for i, name in enumerate(narrow):
                        mm = pe.matmul(psB[:, 0:NB * cols], nbt[:, half, i, :], D(name), start=i == 0, stop=True,
                                       skip_group_check=True)
                    for j in range(NB if wide else 0):
                        mm = pe.matmul(psB[:, j * cols:(j + 1) * cols], nat[half][0:ka, j * P:(j + 1) * P], W(wide),
                                       start=not narrow, stop=True, skip_group_check=True)
                    mm.then_inc(product_done, 1)

                def batch(turn, half, last=False):
                    k = turn * 2 + half
                    pe.wait_ge(turned_out, k + (n * BATCHES + 1))
                    if not (last and half):
                        turn_batch(k + 1, 1 - half)
                    product(k, half)

                turn_batch(0, 0)
                with pe.Fori(0, BATCHES // 2 - 1) as turn:
                    for half in range(2):
                        batch(turn, half)
                for half in range(2):
                    batch(BATCHES // 2 - 1, half, last=True)

            conv(0)
            pe.wait_ge(constants_in, n_constants)
            stage(0, RF, "a1", ["ar1"])
            conv(1)
            stage(1, RF, "a2", ["ar2"])
            conv(2)
            stage(2, RF, "b1", ["br1"], cols=2 * F)
            stage(3, 2 * F, "b2", cols=RF)
            stage(4, 2 * F, "br2")
            conv(3)

            def target_rows(s, turn):
                g = turn * SLOTS + s
                lo = pe.value_load(spans[0:1, bass.ds(g, 1), 0], min_val=0, max_val=WINDOWS - 1)
                more = pe.value_load(spans[0:1, bass.ds(g, 1), 1], min_val=0, max_val=WINDOWS - 1)
                extras = pe.value_load(spans[0:1, bass.ds(g, 1), 2], min_val=0, max_val=GROUPS * WINDOWS)

                def pair(columns, win, first):
                    for t in range(G):
                        mm = pe.matmul(row_parts[:, t // HALF, t % HALF, :, :].rearrange("p k f -> p (k f)"),
                                       columns[:, t * P:(t + 1) * P],
                                       hparts[:, bass.ds(win, 1), :, :].rearrange("p w k f -> p (w k f)"),
                                       start=first and t % HALF == 0, stop=True, skip_group_check=True)
                    return mm

                pe.wait_ge(target_ready, g + 1)
                pair(target, lo, True).then_inc(target_used, 1)
                with pe.If(more > 0):
                    with pe.Fori(1, more + 1) as i:
                        pe.wait_ge(extra_ready, extras + i)
                        pair(extra_target, within(lo + i, WINDOWS - 1), False).then_inc(extra_used, 1)

            def turn_outer(s, turn):
                pe.wait_ge(expanded_ready[s], turn + (TP * TURNS + 2))
                for t in range(G):
                    mm = pe.transpose(psA[:, t * P:(t + 1) * P], outer[:, t * P:(t + 1) * P], ident[:, :])
                mm.then_inc(outer_turned, 1)

            def messages(s, turn, last=False):
                after = (s + 1) % SLOTS, turn + (s + 1) // SLOTS
                if not last:
                    target_rows(*after)
                pe.wait_ge(outer_out, turn * SLOTS + s + 1)
                for t in range(G):
                    mm = pe.matmul(psB[:, t * F:(t + 1) * F], outerT[:, t * P:(t + 1) * P], W("mtp"), start=True, stop=True)
                mm.then_inc(msg_product, 1)
                if not last:
                    turn_outer(*after)
                pe.wait_ge(parts_ready, turn * SLOTS + s + 1)
                pe.wait_ge(same_ready, turn * SLOTS + s + 1)
                for t in range(G):
                    for k in range(PARTS):
                        mm = pe.matmul(psC[:, t * F:(t + 1) * F], same[:, t, :], msg_parts[:, k, t * F:(t + 1) * F],
                                       start=t == 0 and k == 0, stop=True, skip_group_check=True)
                mm.then_inc(same_summed, 1)

            pe.sem_inc(extra_used)
            target_rows(0, 0)
            turn_outer(0, 0)
            with pe.Fori(0, TURNS - 1) as turn:
                for s in range(SLOTS):
                    messages(s, turn)
            for s in range(SLOTS):
                messages(s, TURNS - 1, last=s == SLOTS - 1)
            stage(5, narrow=["mlin"])
            stage(6, RF, "utp0")
            stage(7, RF, "utp1")
            stage(8, narrow=["ulin"])
            conv(5)
            stage(9, RF, "emb")
            stage(10, narrow=["gi", "gh"], cols=4 * F)

        @block.vector
        def _(dve):
            steps, asked = [0], [0]

            def step(ins):
                steps[0] += 1
                ins.then_inc(dve_steps, 1)
                dve.wait_ge(dve_steps, steps[0])

            def ask(ins):
                asked[0] += 1
                ins.then_inc(act_asked, 1)
                dve.wait_ge(act_done, asked[0])

            def over(ap, n):
                return ap.unsqueeze(2).to_broadcast([P, ap.shape[1], n])

            def cols(t, k):
                return t[:, 0:WINDOWS * k].rearrange("p (w k) -> p w k", k=k)

            x3 = xs[:, :, :]
            h3, h32 = cols(hs, F), cols(hs, 2 * F)
            t3, t32 = cols(ta, F), cols(ta, 2 * F)
            u3 = cols(tb, F)
            S4 = S[:, 0:WINDOWS, 0:RF].rearrange("p w (r f) -> p w r f", r=R)

            def settle():
                step(dve.tensor_copy(none[:, :], spare[:, :]))

            def layernorm():
                step(dve.tensor_reduce(stat[:, 0, :], x3, AX.X, ALU.add))
                step(dve.tensor_scalar(stat[:, 0, :], stat[:, 0, :], 1.0 / F, None, ALU.mult))
                step(dve.tensor_tensor(t3, x3, over(stat[:, 0, :], F), ALU.subtract))
                step(dve.tensor_tensor(u3, t3, t3, ALU.mult))
                step(dve.tensor_reduce(stat[:, 1, :], u3, AX.X, ALU.add))
                ask(dve.tensor_scalar(stat[:, 1, :], stat[:, 1, :], 1.0 / F, EPS, ALU.mult, ALU.add))
                step(dve.reciprocal(stat[:, 0, :], stat[:, 1, :]))
                step(dve.tensor_tensor(t3, t3, over(stat[:, 0, :], F), ALU.mult))
                dve.tensor_scalar(h3, t3, 0.0, None, ALU.max).then_inc(h_ready, 1)

            def clear_sums():
                step(dve.memset(flatS, 0.0))

            def split_rows():
                settle()
                step(dve.tensor_copy(hparts[:, 0:WINDOWS, 0, :], h3))
                step(dve.tensor_tensor(t3, h3, hparts[:, 0:WINDOWS, 0, :], ALU.subtract))
                step(dve.tensor_copy(hparts[:, 0:WINDOWS, 1, :], t3))
                step(dve.tensor_tensor(hparts[:, 0:WINDOWS, 2, :], t3, hparts[:, 0:WINDOWS, 1, :], ALU.subtract))

            def expand(p, s, turn):
                dve.wait_ge(rows_in[CONV.index(p) // 3][s], turn * landed(p) + (landed(p) + landed_before(p)))
                dve.tensor_tensor(expanded[:, s % 2, :, RF:SW], over(rec[:, s, TYPE, :], R),
                                  iota_r[:, :].unsqueeze(1).to_broadcast([P, G, R]), ALU.is_equal).then_inc(masks_ready, 1)
                dve.wait_ge(masks_ready, turn * SLOTS + (CONV.index(p) * GROUPS + s + 1))
                dve.tensor_tensor(expanded[:, s % 2, :, 0:RF].rearrange("p t (r f) -> p t r f", r=R),
                                  rows[:, s, :, :].unsqueeze(2).to_broadcast([P, G, R, F]),
                                  expanded[:, s % 2, :, RF:SW].unsqueeze(3).to_broadcast([P, G, R, F]),
                                  ALU.mult).then_inc(expanded_ready[s], 1)

            def frame_columns(s, ready):
                dve.tensor_tensor(onehot[:, :, :], frame[:, :].unsqueeze(1).to_broadcast([P, G, P]),
                                  over(rec[:, s, DST, :], P), ALU.is_equal).then_inc(ready, 1)

            def first_frame(p, g, s):
                dve.tensor_scalar(wraps[:, :], iota_n[:, :], low_place[:, bass.ds(g, 1)], float(P), ALU.is_lt, ALU.mult
                                  ).then_inc(frame_steps[p], 1)
                dve.wait_ge(frame_steps[p], g * 2 + 1)
                dve.scalar_tensor_tensor(out=frame[:, :], in0=wraps[:, :], scalar=low_window[:, bass.ds(g, 1)],
                                         in1=iota_n[:, :], op0=ALU.add, op1=ALU.add).then_inc(frame_steps[p], 1)
                dve.wait_ge(frame_steps[p], g * 2 + 2)
                frame_columns(s, first_ready[p])

            def next_frame(p, s, k):
                dve.tensor_scalar(frame[:, :], frame[:, :], float(P), None, ALU.add).then_inc(more_frames[p], 1)
                dve.wait_ge(more_frames[p], k)
                frame_columns(s, more_ready[p])

            def add_frame(p, g, win, done, k):
                width = SW if p == 0 else RF
                dve.wait_ge(done[p], k)
                for window, mask in ((win, kept), (win + 1, wrapped)):
                    at = S[:, bass.ds(window, 1), 0:width].rearrange("p a b -> p (a b)")
                    dve.scalar_tensor_tensor(out=at, in0=psC[:, 0:width], scalar=mask[:, bass.ds(g, 1)], in1=at,
                                             op0=ALU.mult, op1=ALU.add)

            def places_of(p, s, turn):
                dve.wait_ge(place_in[s], turn * 16 + 16 * (hybrid(p) * TURNS + 1))
                for way in range(WAYS):
                    ins = dve.tensor_scalar(fine[:, s % 2, way, :], place[:, s, :], node_of[:, way:way + 1], None, ALU.is_equal)
                ins.then_inc(fine_ready, 1)

            def pick(p, s, turn):
                k = (turn * SLOTS + (hybrid(p) * GROUPS + s)) * 2
                dve.wait_ge(rec_in[s], turn * 16 + 16 * (p * TURNS + 1))
                dve.tensor_tensor(block_of[:, :, :], over(rec[:, s, BLOCK, G - OWN:G], BLOCKS),
                                  iota_n[:, 0:BLOCKS].unsqueeze(1).to_broadcast([P, OWN, BLOCKS]), ALU.is_equal).then_inc(pick_steps, 1)
                dve.wait_ge(pick_steps, k + 1)
                dve.wait_ge(own_gathered, turn * SLOTS + (hybrid(p) * GROUPS + s + 1))
                for t in range(0, OWN, 2):
                    n = min(2, OWN - t)
                    at = s % 2 * 1024 + t // 2 * 512
                    ins = dve.tensor_tensor(picked[:, t:t + n, :, :],
                                            psA[:, at:at + n * BLOCKS * F].rearrange("p (t b f) -> p t b f", t=n, f=F),
                                            block_of[:, t:t + n, :].unsqueeze(3).to_broadcast([P, n, BLOCKS, F]), ALU.mult)
                ins.then_inc(pick_steps, 1)
                dve.wait_ge(pick_steps, k + 2)
                dve.tensor_reduce(rows[:, s, G - OWN:G, :], picked[:, :, :, :].rearrange("p t b f -> p t f b"), AX.X, ALU.add)

            def conv(p):
                def group(s, turn, last=False):
                    g = turn * SLOTS + s
                    lo = dve.value_load(spans[0:1, bass.ds(g, 1), 0], min_val=0, max_val=WINDOWS - 1)
                    more = dve.value_load(spans[0:1, bass.ds(g, 1), 3], min_val=0, max_val=WINDOWS - 1)
                    extras = dve.value_load(spans[0:1, bass.ds(g, 1), 4], min_val=0, max_val=GROUPS * WINDOWS)
                    first_frame(p, g, s)
                    if own(p) and not (last and s >= 2):
                        places_of(p, (s + 2) % SLOTS, turn + (s + 2) // SLOTS)
                    if not (last and s == SLOTS - 1):
                        after = (s + 1) % SLOTS, turn + (s + 1) // SLOTS
                        if own(p):
                            pick(p, *after)
                        expand(p, *after)
                    add_frame(p, g, lo, first_done, g + 1)
                    with dve.If(more > 0):
                        with dve.Fori(1, more + 1) as i:
                            next_frame(p, s, extras + i)
                            add_frame(p, g, within(lo + i, WINDOWS - 1), more_done, extras + i)
                    dve.sem_inc(slot_free[s])

                if own(p):
                    split_rows()
                    places_of(p, 0, 0)
                    places_of(p, 1, 0)
                    pick(p, 0, 0)
                expand(p, 0, 0)
                with dve.Fori(0, TURNS - 1) as turn:
                    for s in range(SLOTS):
                        group(s, turn)
                for s in range(SLOTS):
                    group(s, TURNS - 1, last=True)

            def stage(n, load, narrow, store, width):
                def operands(k, half):
                    for i, t in enumerate(narrow):
                        laid = dve.tensor_copy(nb[:, half, i, :].rearrange("p (w k) -> p w k", w=NB), batch(t, k * NB))
                    if load:
                        laid = load(k * NB, na[half])
                    laid.then_inc(operands_ready, 1)

                def result(turn, half, last=False):
                    k = turn * 2 + half
                    if not last:
                        dve.wait_ge(turned, k + (n * BATCHES + 1))
                        operands(k + 2, half)
                    dve.wait_ge(product_done, k + (n * BATCHES + 1))
                    store(k * NB, psB[:, 0:NB * width].rearrange("p (w k) -> p w k", k=width)).then_inc(batch_done, 1)

                for half in range(2):
                    operands(half, half)
                with dve.Fori(0, BATCHES // 2 - 1) as turn:
                    for half in range(2):
                        result(turn, half)
                for half in range(2):
                    result(BATCHES // 2 - 1, half, last=True)

            def batch(t, w0):
                return t[:, w0:w0 + NB, :] if isinstance(w0, int) else t[:, bass.ds(w0, NB), :]

            def from_sums(w0, to):
                return dve.tensor_tensor(to.rearrange("p (w r f) -> p w r f", w=NB, r=R), batch(S[:, :, 0:RF], w0).rearrange(
                    "p w (r f) -> p w r f", r=R), batch(inv, w0).unsqueeze(3).to_broadcast([P, NB, R, F]), ALU.mult)

            def from_plain_sums(w0, to):
                return dve.tensor_copy(to.rearrange("p (w k) -> p w k", w=NB), batch(S[:, :, 0:RF], w0))

            def from_tile(t, k):
                return lambda w0, to: dve.tensor_copy(to[:, 0:NB * k].rearrange("p (w k) -> p w k", w=NB), batch(t, w0))

            def plus(t, k, bias):
                return lambda w0, psum: dve.tensor_tensor(batch(t, w0), psum, bias.unsqueeze(1).to_broadcast([P, NB, k]), ALU.add)

            def times(t, scale):
                return lambda w0, psum: dve.tensor_scalar(batch(t, w0), psum, scale, None, ALU.mult)

            dve.memset(xs[:, WINDOWS - 1, :], 0.0).then_inc(cleared, 1)
            dve.memset(diagonal[:, :], 0.0).then_inc(cleared, 1)
            dve.memset(span[:, 3, :], 1.0)

            dve.memset(hparts[:, WINDOWS:, :, :], 0.0)
            masked = hs[:, :].bitcast(I32)
            dve.wait_ge(flat_in, 16)
            step(dve.tensor_scalar(masked, ta[:, :].bitcast(I32), WAYS * P - 1, None, ALU.bitwise_and))
            dve.tensor_copy(tb[:, :].bitcast(I16), masked).then_inc(places_built, 1)

            dve.wait_ge(iotas, 8)
            for c in range(CHUNKS):
                dve.wait_ge(edges_in[c], 48)
                e = edge_chunk(c)
                r = record_chunk(c)
                if c >= 2:
                    dve.wait_ge(records_out[c - 2], 16)
                ev = e.rearrange("p k (g t) -> p k g t", t=G)
                dve.tensor_scalar(r[:, :, SRC_ROW, :], ev[:, 0], P - 1, None, ALU.bitwise_and)
                step(dve.tensor_scalar(r[:, :, TYPE_ROW, :], ev[:, 0], 7, None, ALU.logical_shift_right))
                step(dve.tensor_reduce(ext[:, 0, c * CG:(c + 1) * CG], ev[:, 1], AX.X, ALU.max))
                step(dve.tensor_reduce(ext[:, 1, c * CG:(c + 1) * CG], ev[:, 1], AX.X, ALU.min))
                step(dve.scalar_tensor_tensor(out=r[:, :, SRC_ROW, :], in0=r[:, :, SRC_ROW, :], scalar=float(WINDOWS),
                                              in1=r[:, :, TYPE_ROW, :], op0=ALU.mult, op1=ALU.add))
                dve.scalar_tensor_tensor(out=r[:, :, TYPE_ROW, :], in0=r[:, :, SRC_ROW, :], scalar=float(R),
                                         in1=ev[:, 2], op0=ALU.mult, op1=ALU.add)
                dve.tensor_scalar(r[:, :, BLOCK, :], ev[:, 0], 10, None, ALU.logical_shift_right)
                dve.tensor_copy(r[:, :, DST, :], ev[:, 1])
                dve.tensor_copy(r[:, :, TYPE, :], ev[:, 2])
                dve.tensor_copy(r[:, :, SRC, :], ev[:, 0]).then_inc(records_built, 1)
            step(dve.tensor_scalar(ext[:, 1, :], ext[:, 1, :], -1.0, None, ALU.mult))
            dve.tensor_copy(none[:, :], spare[:, :]).then_inc(ext_ready, 1)
            for c in range(CHUNKS):
                dve.wait_ge(records_out[c], 16)
            dve.wait_ge(places_out, 16)
            dve.memset(flatS, 0.0).then_inc(cleared, 1)

            dve.wait_ge(extr_ready, 1)
            step(dve.tensor_scalar(extr[:, 1, :], extr[:, 1, :], -1.0, None, ALU.mult))
            step(dve.tensor_copy(lowest[:, :], extr[:, 1, :]))
            step(dve.tensor_scalar(lowest[:, :], lowest[:, :], P - 1, None, ALU.bitwise_and))
            step(dve.tensor_copy(low_place[:, :], lowest[:, :]))
            dve.tensor_tensor(low_window[:, :], extr[:, 1, :], low_place[:, :], ALU.subtract)
            dve.tensor_scalar(wrapped[:, :], low_place[:, :], node_of[:, 0:1], None, ALU.is_gt)
            dve.tensor_scalar(kept[:, :], low_place[:, :], node_of[:, 0:1], None, ALU.is_le)

            dve.tensor_copy(span_of[:, 0, :], extr[0:1, 1, :])
            dve.tensor_copy(span_of[:, 1, :], extr[0:1, 0, :])
            step(dve.tensor_tensor(span_of[:, 2, :], extr[0:1, 0, :], extr[0:1, 1, :], ALU.subtract))
            step(dve.tensor_scalar(span_of[:, :, :], span_of[:, :, :], 7, None, ALU.logical_shift_right))
            dve.tensor_copy(span[:, 0, :], span_of[:, 0, :])
            step(dve.tensor_copy(span[:, 1, :], span_of[:, 1, :]))
            dve.tensor_copy(spans[:, :, 0], span[:, 0, :])
            step(dve.tensor_tensor(span[:, 1, :], span[:, 1, :], span[:, 0, :], ALU.subtract))
            for at in (1, 3):
                step(dve.tensor_tensor_scan(span[:, 2, :], span[:, 3, :], span[:, 1, :], 0.0, ALU.mult, ALU.add))
                step(dve.tensor_tensor(span[:, 2, :], span[:, 2, :], span[:, 1, :], ALU.subtract))
                dve.tensor_copy(spans[:, :, at], span[:, 1, :])
                step(dve.tensor_copy(spans[:, :, at + 1], span[:, 2, :]))
                if at == 1:
                    step(dve.tensor_copy(span[:, 1, :], span_of[:, 2, :]))
            dve.tensor_copy(none[:, :], spare[:, :]).then_inc(spans_ready, 1)
            dve.wait_ge(spans_ready, 1)

            dve.wait_ge(x_in, 32)
            layernorm()
            dve.wait_ge(sums_zero, 16 * G)

            conv(0)
            settle()
            step(dve.tensor_scalar(inv[:, :, :], S[:, 0:WINDOWS, RF:SW], 1.0, None, ALU.max))
            step(dve.reciprocal(inv[:, :, :], inv[:, :, :]))
            dve.wait_ge(constants_in, n_constants)
            stage(0, from_sums, [h3], plus(t3, F, B("ab1")), F)
            settle()
            dve.tensor_scalar(h3, t3, 0.0, None, ALU.max).then_inc(h_ready, 1)
            clear_sums()
            conv(1)
            settle()
            stage(1, from_sums, [h3], plus(t3, F, B("ab2")), F)
            settle()
            step(dve.tensor_reduce(stat[:, 0, :], t3, AX.X, ALU.max))
            step(dve.tensor_tensor(u3, t3, over(stat[:, 0, :], F), ALU.subtract))
            step(dve.tensor_tensor(x3, x3, u3, ALU.add))
            ask(dve.tensor_copy(none[:, :], spare[:, :]))
            ask(dve.tensor_reduce(stat[:, 0, :], t3, AX.X, ALU.add))
            step(dve.tensor_tensor(x3, x3, over(stat[:, 1, :], F), ALU.subtract))
            layernorm()

            clear_sums()
            conv(2)
            settle()
            stage(2, from_sums, [h3], plus(t32, 2 * F, B("bb1")), 2 * F)
            settle()
            step(dve.tensor_scalar(h32, t32, 0.0, None, ALU.max))
            Y = flatS[:, 0:WINDOWS * RF].rearrange("p (w k) -> p w k", k=RF)
            stage(3, from_tile(h32, 2 * F), [], lambda w0, psum: dve.tensor_copy(batch(Y, w0), psum), RF)
            dve.tensor_copy(none[:, :], spare[:, :]).then_inc(h_ready, 1)
            stage(4, from_tile(h32, 2 * F), [], plus(u3, F, B("bb2")), F)
            settle()
            step(dve.tensor_tensor(x3, x3, u3, ALU.add))
            dve.wait_ge(table_out, 16 * 4)
            clear_sums()
            conv(3)
            settle()
            step(dve.tensor_tensor(S4, S4, inv[:, :, :].unsqueeze(3).to_broadcast([P, WINDOWS, R, F]), ALU.mult))
            for r in range(R):
                step(dve.tensor_tensor(x3, x3, S4[:, :, r, :], ALU.add))
            layernorm()

            def targets(s, turn):
                g = turn * SLOTS + s
                lo = dve.value_load(spans[0:1, bass.ds(g, 1), 0], min_val=0, max_val=WINDOWS - 1)
                more = dve.value_load(spans[0:1, bass.ds(g, 1), 1], min_val=0, max_val=WINDOWS - 1)
                extras = dve.value_load(spans[0:1, bass.ds(g, 1), 2], min_val=0, max_val=GROUPS * WINDOWS)

                def pair(columns, win):
                    return dve.tensor_scalar(columns, wide[:, s % 2, 1, :], node_of[:, bass.ds(win, 1)], None, ALU.is_equal)

                dve.wait_ge(wide_in[s % 2], turn * 64 + (s // 2 + 1) * 32)
                pair(target, lo).then_inc(target_ready, 1)
                with dve.If(more > 0):
                    with dve.Fori(1, more + 1) as i:
                        dve.wait_ge(extra_used, extras + i)
                        pair(extra_target, within(lo + i, WINDOWS - 1)).then_inc(extra_ready, 1)
                return extras + more

            def spread(s, turn, extras, first=False):
                dve.wait_ge(target_used, turn * SLOTS + s + 1)
                dve.wait_ge(extra_used, extras + 1)
                dve.wait_ge(attrs_in[s], turn * 16 + 16)
                if not first:
                    dve.wait_ge(outer_turned, turn * SLOTS + s)
                for half in range(2):
                    dve.tensor_reduce(rows[:, s, half * HALF:(half + 1) * HALF, :],
                                      row_parts[:, half].rearrange("p t k f -> p t f k"), AX.X, ALU.add).then_inc(rows_summed, 1)
                dve.wait_ge(rows_summed, (turn * SLOTS + s) * 2 + 2)
                dve.tensor_tensor(outer.rearrange("p (t j f) -> p t j f", t=G, j=R),
                                  rows[:, s, :, :].unsqueeze(2).to_broadcast([P, G, R, F]),
                                  attrs[:, s, :, :].unsqueeze(3).to_broadcast([P, G, R, F]),
                                  ALU.mult).then_inc(expanded_ready[s], 1)

            def same_sources(s, turn, last=False):
                k = turn * SLOTS + s
                after = (s + 1) % SLOTS, turn + (s + 1) // SLOTS
                if not last:
                    extras = targets(*after)
                dve.wait_ge(wide_in[s % 2], turn * 64 + (s // 2 + 1) * 32)
                dve.wait_ge(rec_in[s], turn * 16 + 16 * (TP * TURNS + 1))
                dve.tensor_tensor(same, wide[:, s % 2, 0, :].rearrange("p (t e) -> p t e", t=G),
                                  over(rec[:, s, SRC, :], P), ALU.is_equal).then_inc(same_ready, 1)
                dve.wait_ge(same_ready, k + 1)
                dve.sem_inc(wide_free[s % 2])
                if not last:
                    spread(*after, extras)
                dve.tensor_tensor(earlier, same, before[:, :].unsqueeze(1).to_broadcast([P, G, P]),
                                  ALU.mult).then_inc(dup_steps, 1)
                dve.wait_ge(dup_steps, k * 4 + 1)
                dve.tensor_reduce(dup[:, 0, :], earlier, AX.X, ALU.add)
                dve.tensor_scalar(dup[:, 1, :], rec[:, s, SRC_ROW, :], spare[:, 0:1], -1.0, ALU.subtract,
                                  ALU.mult).then_inc(dup_steps, 1)
                dve.wait_ge(msg_ready, k + 1)
                dve.tensor_copy(msg_parts[:, 0, :], msg[:, s % 2, :]).then_inc(split_steps, 1)
                dve.wait_ge(dup_steps, k * 4 + 2)
                dve.scalar_tensor_tensor(out=dup[:, 2, :], in0=dup[:, 0, :], scalar=0.0, in1=dup[:, 1, :],
                                         op0=ALU.is_gt, op1=ALU.mult).then_inc(dup_steps, 1)
                dve.wait_ge(split_steps, k * 3 + 1)
                dve.tensor_tensor(msg_rest[:, :], msg[:, s % 2, :], msg_parts[:, 0, :], ALU.subtract).then_inc(split_steps, 1)
                dve.wait_ge(dup_steps, k * 4 + 3)
                dve.wait_ge(scatter_free[s], turn + 1)
                dve.tensor_tensor(scat[:, s, :], dup[:, 2, :], rec[:, s, SRC_ROW, :], ALU.add).then_inc(dup_steps, 1)
                dve.wait_ge(split_steps, k * 3 + 2)
                dve.tensor_copy(msg_parts[:, 1, :], msg_rest[:, :]).then_inc(split_steps, 1)
                dve.wait_ge(split_steps, k * 3 + 3)
                dve.tensor_tensor(msg_parts[:, 2, :], msg_rest[:, :], msg_parts[:, 1, :], ALU.subtract).then_inc(parts_ready, 1)
                dve.wait_ge(dup_steps, k * 4 + 4)
                dve.wait_ge(same_summed, k + 1)
                dve.tensor_copy(summed[:, s, :], psC[:, 0:G * F]).then_inc(summed_ready[s], 1)
                dve.sem_inc(slot_free[s])

            split_rows()
            spread(0, 0, targets(0, 0), first=True)
            with dve.Fori(0, TURNS - 1) as turn:
                for s in range(SLOTS):
                    same_sources(s, turn)
            for s in range(SLOTS):
                same_sources(s, TURNS - 1, last=s == SLOTS - 1)
            T8 = flatS[:, 0:(G // 2) * WINDOWS * F].rearrange("p (i k) -> p i k", i=G // 2)
            for half in range(2):
                dve.wait_ge(sums_in[half], 16 * (G // 2))
                for i in range(G // 2):
                    if half == 0 and i == 0:
                        step(dve.tensor_copy(tb[:, :], T8[:, 0, :]))
                    else:
                        step(dve.tensor_tensor(tb[:, :], tb[:, :], T8[:, i, :], ALU.add))
                if half == 0:
                    dve.sem_inc(sums_read)
            stage(5, None, [u3], times(t3, float(F) ** -0.5), F)
            settle()
            Z = flatS[:, 0:WINDOWS * RF].rearrange("p (w i f) -> p w i f", i=R, f=F)
            Z3 = flatS[:, 0:WINDOWS * RF].rearrange("p (w k) -> p w k", k=RF)
            v3 = cols(hs[:, WINDOWS * F:], F)
            for half in range(2):
                step(dve.tensor_tensor(Z, h3[:, :, half * R:(half + 1) * R].unsqueeze(3).to_broadcast([P, WINDOWS, R, F]),
                                       t3.unsqueeze(2).to_broadcast([P, WINDOWS, R, F]), ALU.mult))
                to = (u3, v3)[half]
                stage(6 + half, from_tile(Z3, RF), [], lambda w0, psum, to=to: dve.tensor_copy(batch(to, w0), psum), F)
                settle()
            ask(dve.tensor_tensor(u3, u3, v3, ALU.add))
            stage(8, None, [u3], times(t3, float(F) ** -0.5), F)
            settle()
            step(dve.tensor_tensor(t3, t3, h3, ALU.add))
            step(dve.tensor_tensor(x3, x3, t3, ALU.add))
            layernorm()

            clear_sums()
            dve.tensor_tensor(bg[:, 0:2 * F], B("ih", 0, 2 * F), B("hh", 0, 2 * F), ALU.add)
            dve.tensor_copy(bg[:, 2 * F:3 * F], B("ih", 2 * F))
            step(dve.tensor_copy(bg[:, 3 * F:4 * F], B("hh", 2 * F)))
            conv(5)
            settle()
            stage(9, from_plain_sums, [], times(t3, 1.0), F)
            settle()
            gates = flatS[:, 0:WINDOWS * 4 * F].rearrange("p (w k) -> p w k", k=4 * F)
            stage(10, None, [t3, h3], plus(gates, 4 * F, bg[:, :]), 4 * F)
            ask(dve.tensor_copy(none[:, :], spare[:, :]))
            step(dve.tensor_tensor(t3, gates[:, :, 0:F], gates[:, :, 3 * F:4 * F], ALU.mult))
            ask(dve.tensor_tensor(gates[:, :, 2 * F:3 * F], gates[:, :, 2 * F:3 * F], t3, ALU.add))
            new = gates[:, :, 2 * F:3 * F]
            step(dve.tensor_tensor(t3, h3, new, ALU.subtract))
            step(dve.tensor_tensor(t3, t3, gates[:, :, F:2 * F], ALU.mult))
            step(dve.tensor_tensor(t3, t3, new, ALU.add))
            dve.tensor_tensor(x3, x3, t3, ALU.add).then_inc(out_ready, 1)


def kernel(**inputs):
    import numpy as np
    import concourse.bacc as bacc
    from concourse.bass_utils import run_bass_kernel_spmd

    def edges(name, fill):
        a = np.asarray(inputs[name])
        return np.concatenate([a, np.full((EPAD - EDGES,) + a.shape[1:], fill, a.dtype)])

    def tiles(a):
        return np.ascontiguousarray(a.reshape(EC, P, -1).transpose(1, 0, 2).reshape(P, -1))

    def get(name, shape=None, perm=None):
        a = np.asarray(inputs[name])
        a = a if perm is None else a.transpose(perm)
        return np.ascontiguousarray(a if shape is None else a.reshape(shape))

    none = NPAD - 1
    src, dst = edges("src", none), edges("dst", none)
    arrays = {
        "x": get("x"), "src": tiles(src), "dst": tiles(dst), "typ": tiles(edges("edge_type_8", 0)),
        "src_flat": src, "dst_flat": dst, "attr": tiles(edges("edge_attr_8", 0)),
        "a1": get("L0_gnn_W1", (RF, F)), "ar1": get("L0_gnn_root1"), "a2": get("L0_gnn_W2", (RF, F)), "ar2": get("L0_gnn_root2"),
        "b1": get("L1_gnn_W1", (RF, 2 * F)), "br1": get("L1_gnn_root1"),
        "b2": get("L1_gnn_W2", (2 * F, RF), (1, 0, 2)), "br2": get("L1_gnn_root2"),
        "mtp": get("L2_gnn_W_msg_tp", (RF, F), (1, 0, 2)), "mlin": get("L2_gnn_W_msg_lin"),
        "utp0": get("L2_gnn_W_upd_tp", (F * F, F))[0:RF], "utp1": get("L2_gnn_W_upd_tp", (F * F, F))[RF:],
        "ulin": get("L2_gnn_W_upd_lin"),
        "emb": np.ascontiguousarray(get("L3_gnn_edge_emb", (R, F, F)).transpose(0, 2, 1).reshape(RF, F)),
        "gi": get("L3_gnn_w_ih", None, (1, 0)), "gh": get("L3_gnn_w_hh", None, (1, 0)),
        "ab1": get("L0_gnn_b1"), "ab2": get("L0_gnn_b2"), "bb1": get("L1_gnn_b1"), "bb2": get("L1_gnn_b2"),
        "ih": get("L3_gnn_b_ih"), "hh": get("L3_gnn_b_hh"),
    }
    nc = bacc.Bacc("TRN2", target_bir_lowering=False, num_devices=1)
    d = {n: nc.dram_tensor(f"in_{n}", a.shape, mybir.dt.from_np(a.dtype), kind="ExternalInput").ap() for n, a in arrays.items()}
    out = nc.dram_tensor("out_x", (NODES, F), F32, kind="ExternalOutput").ap()
    gnn_kernel(nc, *(d[n] for n in ("x", "src", "dst", "typ", "src_flat", "dst_flat", "attr")),
               {n: d[n] for n, *_ in WEIGHTS + DIAGONAL}, {n: d[n] for n, _ in BIASES}, out)
    r = run_bass_kernel_spmd(nc, [{f"in_{n}": a for n, a in arrays.items()}], core_ids=[0])
    return r.results[0]["out_x"]
```
